# Optimizing a Trainium2 kernel written in Bass

```python
import numpy as np
import jax
import jax.numpy as jnp

def _softmax(x, axis=-1):
    return jax.nn.softmax(x, axis=axis)

def _gelu(x):
    return jax.nn.gelu(x, approximate=True)

def _silu(x):
    return jax.nn.silu(x)

def _sigmoid(x):
    return jax.nn.sigmoid(x)

def _layernorm(x, axis=-1, eps=1e-05):
    m = jnp.mean(x, axis=axis, keepdims=True)
    v = jnp.var(x, axis=axis, keepdims=True)
    return (x - m) / jnp.sqrt(v + eps)

def _scatter_add(tgt, idx, src, axis=0):
    return tgt.at[idx].add(src)

def _segment_sum(src, seg, n):
    return jax.ops.segment_sum(src, seg, n)
kernel_name = 'mk_decoder_preln_d1_seqx_r4_b5a06d'

def setup_inputs(seed: int=0):
    np.random.seed(seed)
    _w = jnp.asarray

    def _rec_inputs():
        import jax
        import jax.numpy as jnp
        _rk = jax.random.key(seed)
        x = 7.22e-05 + 1 * jax.random.normal(jax.random.fold_in(_rk, 1), (8, 256, 512), jnp.float32)
        _lenS = 256 - jax.random.randint(jax.random.fold_in(_rk, 7), (8,), 0, max(1, 256 // 4) + 1, jnp.int32)
        _lenS2 = 256 - jax.random.randint(jax.random.fold_in(_rk, 8), (8,), 0, max(1, 256 // 4) + 1, jnp.int32)
        _ctx_1024P = jax.random.normal(jax.random.fold_in(_rk, 11), (8, 16, 256), jnp.float32)
        _ctx_1024c = jax.random.dirichlet(jax.random.fold_in(_rk, 511), 0.3 * jnp.ones((16,), jnp.float32), (8, 256))
        _ctx_1024t = jnp.einsum('bsk,bkd->bsd', _ctx_1024c, _ctx_1024P)
        _ctx_1024t = _ctx_1024t * jax.lax.rsqrt(jnp.mean(jnp.square(_ctx_1024t)) + 1e-12) * 0.953939
        ctx_1024 = -1.39393e-06 + 0.999914 * (_ctx_1024t + 0.3 * jax.random.normal(jax.random.fold_in(_rk, 611), (8, 256, 256), jnp.float32))
        fside_BxSx2_0 = jax.random.uniform(jax.random.fold_in(_rk, 12), (8, 256, 2), jnp.float32, 0.0, 0.999707)
        return (x, ctx_1024, fside_BxSx2_0)
    x, ctx_1024, fside_BxSx2_0 = _rec_inputs()

    def _L0_attn_setup():
        import jax, jax.numpy as jnp
        import numpy as np
        HIDDEN = 512
        HEAD_DIM = 64
        N_HEADS = HIDDEN // HEAD_DIM
        ROT_DIM = HEAD_DIM // 2
        THETA = 10000.0
        SCALE_BASE = 512.0
        EPS = 1e-05
        B, S = (1, 512)

        def _rotate_half(t):
            x1 = t[..., 0::2]
            x2 = t[..., 1::2]
            return jnp.stack([-x2, x1], axis=-1).reshape(t.shape)

        def _xpos_rotary(q, k, seqlen):
            dim = ROT_DIM
            inv_freq = 1.0 / THETA ** (jnp.arange(0, dim, 2, dtype=jnp.float32) / dim)
            t = jnp.arange(seqlen, dtype=jnp.float32)
            freqs = t[:, None] * inv_freq[None, :]
            freqs = jnp.repeat(freqs, 2, axis=-1)
            base_scale = (jnp.arange(0, dim, 2, dtype=jnp.float32) + 0.4 * dim) / (1.4 * dim)
            power = (t - seqlen // 2) / SCALE_BASE
            scale = base_scale[None, :] ** power[:, None]
            scale = jnp.concatenate([scale, scale], axis=-1)
            cos, sin = (jnp.cos(freqs), jnp.sin(freqs))

            def apply(x, sc):
                xr, xp = (x[..., :dim], x[..., dim:])
                xr = xr * cos * sc + _rotate_half(xr) * sin * sc
                return jnp.concatenate([xr, xp], axis=-1)
            return (apply(q, scale), apply(k, 1.0 / scale))

        def _msr_forward(x, wqkv, wg, wo, gn_weight, gn_bias):
            b, s, _ = x.shape
            qkv = x @ wqkv.T
            qkv = qkv.reshape(b, s, N_HEADS, 3 * HEAD_DIM).transpose(0, 2, 1, 3)
            q, k, v = jnp.split(qkv, 3, axis=-1)
            q, k = _xpos_rotary(q, k, s)
            gamma = 1.0 - 2.0 ** (-5.0 - jnp.arange(N_HEADS, dtype=jnp.float32))
            idx = jnp.arange(s)
            nm = idx[:, None] - idx[None, :]
            decay = jnp.where(nm >= 0, gamma[:, None, None] ** jnp.maximum(nm, 0).astype(jnp.float32), 0.0)
            scores = jnp.einsum('bhid,bhjd->bhij', q, k) * decay
            ret = jnp.einsum('bhij,bhjd->bhid', scores, v)
            mean = ret.mean(axis=(2, 3), keepdims=True)
            var = ret.var(axis=(2, 3), keepdims=True)
            ret = (ret - mean) / jnp.sqrt(var + EPS)
            ret = ret * gn_weight[None, :, None, None] + gn_bias[None, :, None, None]
            y = ret.transpose(0, 2, 1, 3).reshape(b, s, HIDDEN)
            g = x @ wg.T
            mish = g * jnp.tanh(jax.nn.softplus(g))
            return mish * y @ wo.T
        key = jax.random.key(seed)
        ks = jax.random.split(key, 4)
        std = HIDDEN ** (-0.5)
        x = jax.random.normal(ks[0], (B, S, HIDDEN), jnp.float32)
        wqkv = jax.random.normal(ks[1], (3 * HIDDEN, HIDDEN), jnp.float32) * std
        wg = jax.random.normal(ks[2], (HIDDEN, HIDDEN), jnp.float32) * std
        wo = jax.random.normal(ks[3], (HIDDEN, HIDDEN), jnp.float32) * std
        gn_weight = jnp.ones((N_HEADS,), jnp.float32)
        gn_bias = jnp.zeros((N_HEADS,), jnp.float32)
        return {'x': x, 'wqkv': wqkv, 'wg': wg, 'wo': wo, 'gn_weight': gn_weight, 'gn_bias': gn_bias}
    _L0_attn_all = _L0_attn_setup()
    _L0_attn_in = {k: v for k, v in _L0_attn_all.items() if k in ('wqkv', 'wg', 'wo', 'gn_weight', 'gn_bias')}
    del _L0_attn_all

    def _L0_xattn_setup():
        import jax, jax.numpy as jnp
        import numpy as np
        DIM = 512
        CTX_DIM = 256
        N_HEADS = 32
        HEAD_DIM = DIM // N_HEADS
        POS_DIM = 2
        B, N, CTXN = (2, 512, 512)
        ROPE_BASE = 10000.0

        def apply_axial_rope(x, pos):
            b, n, h, d = x.shape
            p = pos.shape[-1]
            dpa = d // p
            half = dpa // 2
            freqs = ROPE_BASE ** (-jnp.arange(half, dtype=x.dtype) / half)
            ang = pos[..., :, None] * freqs
            cos = jnp.cos(ang)[:, :, None, :, :]
            sin = jnp.sin(ang)[:, :, None, :, :]
            xr = x.reshape(b, n, h, p, half, 2)
            x1, x2 = (xr[..., 0], xr[..., 1])
            out = jnp.stack([x1 * cos - x2 * sin, x1 * sin + x2 * cos], axis=-1)
            return out.reshape(b, n, h, d)
        key = jax.random.key(seed)
        ks = jax.random.split(key, 8)
        x = jax.random.normal(ks[0], (B, N, DIM), jnp.float32)
        ctx = jax.random.normal(ks[1], (B, CTXN, CTX_DIM), jnp.float32)
        pos_map = jax.random.uniform(ks[2], (B, N, POS_DIM), jnp.float32)
        ctx_pos_map = jax.random.uniform(ks[3], (B, CTXN, POS_DIM), jnp.float32)
        Wq = jax.random.normal(ks[4], (DIM, DIM), jnp.float32) / np.sqrt(DIM)
        Wkv = jax.random.normal(ks[5], (CTX_DIM, 2 * DIM), jnp.float32) / np.sqrt(CTX_DIM)
        Wout = jax.random.normal(ks[6], (DIM, DIM), jnp.float32) / np.sqrt(DIM)
        bout = jnp.zeros((DIM,), jnp.float32)
        return {'x': x, 'ctx': ctx, 'pos_map': pos_map, 'ctx_pos_map': ctx_pos_map, 'Wq': Wq, 'Wkv': Wkv, 'Wout': Wout, 'bout': bout}
    _L0_xattn_all = _L0_xattn_setup()
    _L0_xattn_in = {k: v for k, v in _L0_xattn_all.items() if k in ('Wq', 'Wkv', 'Wout', 'bout')}
    del _L0_xattn_all

    def _L0_ffn_setup():
        import jax, jax.numpy as jnp
        import numpy as np
        B, T, C = (2, 256, 512)
        E, TOPK = (8, 2)
        F_MOE = 352
        F_SHARED = 1408
        key = jax.random.key(seed)
        ks = jax.random.split(key, 9)
        s = 0.02
        return {'x': jax.random.normal(ks[0], (B, T, C), dtype=jnp.float32), 'gate_w': jax.random.normal(ks[1], (E, C), dtype=jnp.float32) * s, 'expert_fc1': jax.random.normal(ks[2], (E, F_MOE, C), dtype=jnp.float32) * s, 'expert_fc2': jax.random.normal(ks[3], (E, F_MOE, C), dtype=jnp.float32) * s, 'expert_proj': jax.random.normal(ks[4], (E, C, F_MOE), dtype=jnp.float32) * s, 'shared_fc1': jax.random.normal(ks[5], (F_SHARED, C), dtype=jnp.float32) * s, 'shared_fc2': jax.random.normal(ks[6], (F_SHARED, C), dtype=jnp.float32) * s, 'shared_proj': jax.random.normal(ks[7], (C, F_SHARED), dtype=jnp.float32) * s, 'shared_gate_w': jax.random.normal(ks[8], (1, C), dtype=jnp.float32) * s}
    _L0_ffn_all = _L0_ffn_setup()
    _L0_ffn_in = {k: v for k, v in _L0_ffn_all.items() if k in ('gate_w', 'expert_fc1', 'expert_fc2', 'expert_proj', 'shared_fc1', 'shared_fc2', 'shared_proj', 'shared_gate_w')}
    del _L0_ffn_all
    return {'x': x, 'ctx_1024': ctx_1024, 'fside_BxSx2_0': fside_BxSx2_0, 'L0_attn_wqkv': _L0_attn_in['wqkv'], 'L0_attn_wg': _L0_attn_in['wg'], 'L0_attn_wo': _L0_attn_in['wo'], 'L0_attn_gn_weight': _L0_attn_in['gn_weight'], 'L0_attn_gn_bias': _L0_attn_in['gn_bias'], 'L0_xattn_Wq': _L0_xattn_in['Wq'], 'L0_xattn_Wkv': _L0_xattn_in['Wkv'], 'L0_xattn_Wout': _L0_xattn_in['Wout'], 'L0_xattn_bout': _L0_xattn_in['bout'], 'L0_ffn_gate_w': _L0_ffn_in['gate_w'], 'L0_ffn_expert_fc1': _L0_ffn_in['expert_fc1'], 'L0_ffn_expert_fc2': _L0_ffn_in['expert_fc2'], 'L0_ffn_expert_proj': _L0_ffn_in['expert_proj'], 'L0_ffn_shared_fc1': _L0_ffn_in['shared_fc1'], 'L0_ffn_shared_fc2': _L0_ffn_in['shared_fc2'], 'L0_ffn_shared_proj': _L0_ffn_in['shared_proj'], 'L0_ffn_shared_gate_w': _L0_ffn_in['shared_gate_w']}

def reference(x, ctx_1024, fside_BxSx2_0, L0_attn_wqkv, L0_attn_wg, L0_attn_wo, L0_attn_gn_weight, L0_attn_gn_bias, L0_xattn_Wq, L0_xattn_Wkv, L0_xattn_Wout, L0_xattn_bout, L0_ffn_gate_w, L0_ffn_expert_fc1, L0_ffn_expert_fc2, L0_ffn_expert_proj, L0_ffn_shared_fc1, L0_ffn_shared_fc2, L0_ffn_shared_proj, L0_ffn_shared_gate_w):
    import jax
    import jax.numpy as jnp

    def _L0_attn_ref(x, wqkv, wg, wo, gn_weight, gn_bias):
        import jax, jax.numpy as jnp
        import numpy as np
        HIDDEN = 512
        HEAD_DIM = 64
        N_HEADS = HIDDEN // HEAD_DIM
        ROT_DIM = HEAD_DIM // 2
        THETA = 10000.0
        SCALE_BASE = 512.0
        EPS = 1e-05
        B, S = (1, 512)

        def _rotate_half(t):
            x1 = t[..., 0::2]
            x2 = t[..., 1::2]
            return jnp.stack([-x2, x1], axis=-1).reshape(t.shape)

        def _xpos_rotary(q, k, seqlen):
            dim = ROT_DIM
            inv_freq = 1.0 / THETA ** (jnp.arange(0, dim, 2, dtype=jnp.float32) / dim)
            t = jnp.arange(seqlen, dtype=jnp.float32)
            freqs = t[:, None] * inv_freq[None, :]
            freqs = jnp.repeat(freqs, 2, axis=-1)
            base_scale = (jnp.arange(0, dim, 2, dtype=jnp.float32) + 0.4 * dim) / (1.4 * dim)
            power = (t - seqlen // 2) / SCALE_BASE
            scale = base_scale[None, :] ** power[:, None]
            scale = jnp.concatenate([scale, scale], axis=-1)
            cos, sin = (jnp.cos(freqs), jnp.sin(freqs))

            def apply(x, sc):
                xr, xp = (x[..., :dim], x[..., dim:])
                xr = xr * cos * sc + _rotate_half(xr) * sin * sc
                return jnp.concatenate([xr, xp], axis=-1)
            return (apply(q, scale), apply(k, 1.0 / scale))

        def _msr_forward(x, wqkv, wg, wo, gn_weight, gn_bias):
            b, s, _ = x.shape
            qkv = x @ wqkv.T
            qkv = qkv.reshape(b, s, N_HEADS, 3 * HEAD_DIM).transpose(0, 2, 1, 3)
            q, k, v = jnp.split(qkv, 3, axis=-1)
            q, k = _xpos_rotary(q, k, s)
            gamma = 1.0 - 2.0 ** (-5.0 - jnp.arange(N_HEADS, dtype=jnp.float32))
            idx = jnp.arange(s)
            nm = idx[:, None] - idx[None, :]
            decay = jnp.where(nm >= 0, gamma[:, None, None] ** jnp.maximum(nm, 0).astype(jnp.float32), 0.0)
            scores = jnp.einsum('bhid,bhjd->bhij', q, k) * decay
            ret = jnp.einsum('bhij,bhjd->bhid', scores, v)
            mean = ret.mean(axis=(2, 3), keepdims=True)
            var = ret.var(axis=(2, 3), keepdims=True)
            ret = (ret - mean) / jnp.sqrt(var + EPS)
            ret = ret * gn_weight[None, :, None, None] + gn_bias[None, :, None, None]
            y = ret.transpose(0, 2, 1, 3).reshape(b, s, HIDDEN)
            g = x @ wg.T
            mish = g * jnp.tanh(jax.nn.softplus(g))
            return mish * y @ wo.T
        return _msr_forward(x, wqkv, wg, wo, gn_weight, gn_bias)

    def _L0_xattn_ref(x, ctx, pos_map, ctx_pos_map, Wq, Wkv, Wout, bout):
        import jax, jax.numpy as jnp
        import numpy as np
        DIM = 512
        CTX_DIM = 256
        N_HEADS = 32
        HEAD_DIM = DIM // N_HEADS
        POS_DIM = 2
        B, N, CTXN = (2, 512, 512)
        ROPE_BASE = 10000.0

        def apply_axial_rope(x, pos):
            b, n, h, d = x.shape
            p = pos.shape[-1]
            dpa = d // p
            half = dpa // 2
            freqs = ROPE_BASE ** (-jnp.arange(half, dtype=x.dtype) / half)
            ang = pos[..., :, None] * freqs
            cos = jnp.cos(ang)[:, :, None, :, :]
            sin = jnp.sin(ang)[:, :, None, :, :]
            xr = x.reshape(b, n, h, p, half, 2)
            x1, x2 = (xr[..., 0], xr[..., 1])
            out = jnp.stack([x1 * cos - x2 * sin, x1 * sin + x2 * cos], axis=-1)
            return out.reshape(b, n, h, d)
        b, n, _ = x.shape
        ctx_n = ctx.shape[1]
        q = (x @ Wq).reshape(b, n, N_HEADS, HEAD_DIM)
        k, v = jnp.split(ctx @ Wkv, 2, axis=-1)
        k = k.reshape(b, ctx_n, N_HEADS, HEAD_DIM)
        v = v.reshape(b, ctx_n, N_HEADS, HEAD_DIM)
        q = apply_axial_rope(q, pos_map)
        k = apply_axial_rope(k, ctx_pos_map)
        scale = 1.0 / np.sqrt(HEAD_DIM).astype(np.float32)
        logits = jnp.einsum('bqhd,bkhd->bhqk', q, k) * scale
        w = jax.nn.softmax(logits, axis=-1)
        attn = jnp.einsum('bhqk,bkhd->bqhd', w, v)
        attn = attn.reshape(b, n, N_HEADS * HEAD_DIM)
        return attn @ Wout + bout

    def _L0_ffn_ref(x, gate_w, expert_fc1, expert_fc2, expert_proj, shared_fc1, shared_fc2, shared_proj, shared_gate_w):
        import jax, jax.numpy as jnp
        import numpy as np
        B, T, C = (2, 256, 512)
        E, TOPK = (8, 2)
        F_MOE = 352
        F_SHARED = 1408
        b, t, c = x.shape
        xf = x.reshape(-1, c)
        n = xf.shape[0]
        router = xf @ gate_w.T
        probs = jax.nn.softmax(router.astype(jnp.float32), axis=1).astype(x.dtype)
        top_p, top_i = jax.lax.top_k(probs, TOPK)
        combine = jnp.zeros((n, E), dtype=x.dtype).at[jnp.arange(n)[:, None], top_i].set(top_p)
        h1 = jnp.einsum('nc,efc->enf', xf, expert_fc1)
        h2 = jnp.einsum('nc,efc->enf', xf, expert_fc2)
        h = jax.nn.silu(h1) * h2
        out_e = jnp.einsum('enf,ecf->enc', h, expert_proj)
        y = jnp.einsum('ne,enc->nc', combine, out_e)
        s1 = xf @ shared_fc1.T
        s2 = xf @ shared_fc2.T
        shared = jax.nn.silu(s1) * s2 @ shared_proj.T
        y = y + jax.nn.sigmoid(xf @ shared_gate_w.T) * shared
        return y.reshape(b, t, c)
    x = x + _L0_attn_ref(_layernorm(x, axis=-1), L0_attn_wqkv, L0_attn_wg, L0_attn_wo, L0_attn_gn_weight, L0_attn_gn_bias)
    x = x + _L0_xattn_ref(_layernorm(x, axis=-1), ctx_1024, fside_BxSx2_0, fside_BxSx2_0, L0_xattn_Wq, L0_xattn_Wkv, L0_xattn_Wout, L0_xattn_bout)
    x = x + _L0_ffn_ref(_layernorm(x, axis=-1), L0_ffn_gate_w, L0_ffn_expert_fc1, L0_ffn_expert_fc2, L0_ffn_expert_proj, L0_ffn_shared_fc1, L0_ffn_shared_fc2, L0_ffn_shared_proj, L0_ffn_shared_gate_w)
    return x

_drawn_inputs = setup_inputs


def setup_inputs(seed=0):
    import zlib

    import numpy as np

    out = dict(_drawn_inputs(seed))
    spreads = {'L0_attn_gn_weight': (1.0, 0.2),
     'L0_attn_gn_bias': (0.0, 0.1),
     'L0_xattn_bout': (0.0, 0.1)}
    factors = {'L0_ffn_gate_w': 7.543,
     'L0_ffn_expert_fc1': 6.499,
     'L0_ffn_expert_fc2': 6.367,
     'L0_ffn_expert_proj': 6.382,
     'L0_ffn_shared_gate_w': 64.0,
     'L0_ffn_shared_fc1': 8.0,
     'L0_ffn_shared_fc2': 8.0,
     'L0_ffn_shared_proj': 8.0}
    for name, (base, spread) in spreads.items():
        noise = np.random.default_rng([zlib.crc32(name.encode()), seed]).standard_normal(out[name].shape)
        drawn = base * np.exp(spread * noise) if base else spread * noise
        out[name] = jnp.asarray(drawn.astype(out[name].dtype))
    for name, factor in factors.items():
        out[name] = (out[name] * factor).astype(out[name].dtype)
    return out
```

```python
from contextlib import ExitStack

import concourse.bass as bass
import numpy as np
from concourse import mybir

FP32 = mybir.dt.float32
FP32R = mybir.dt.float32r
ALU = mybir.AluOpType
ACT = mybir.ActivationFunctionType
AX = mybir.AxisListType

P = 128
B, S, C = 8, 256, 512
NT = B * S // P
TB = S // P
KT = C // P
EPS = 1e-5

RH, RD, ROT = 8, 64, 32
XH, XD, CTXW = 32, 16, 256
CKT = CTXW // P
E, FE, FS = 8, 352, 1408
GATES = E + 1
FT = (E * FE + FS) // P


def as_f32(ap):
    return ap.bitcast(FP32)


def matmul3(nc, out, left, right, start, stop):
    (lh, ll), (rh, rl) = left, right
    nc.tensor.matmul(out, ll, rh, start=start, stop=False)
    nc.tensor.matmul(out, lh, rl, start=False, stop=False)
    return nc.tensor.matmul(out, lh, rh, start=False, stop=stop)


class Chain:

    def __init__(self, engine, sem, per=0, turn=0, base=0):
        self.engine, self.sem, self.per, self.turn, self.base, self.n = engine, sem, per, turn, base, 0

    def step(self, instruction):
        instruction.then_inc(self.sem, 1)
        self.n += 1
        self.engine.wait_ge(self.sem, self.turn * self.per + (self.base + self.n))


def retention(nc, X, x_dram, wa_dram, decay_dram, rot_dram, gn_dram, blk_dram, ident, ident_dram):
    with ExitStack() as mem:
        def sb(name, shape, dt=FP32):
            return mem.enter_context(nc.sbuf_tensor("a_" + name, shape, dt))

        def sem(name):
            return nc.alloc_semaphore("a_" + name)

        with nc.sbuf_tensor("a_raw", [P, 2, 2048], FP32) as raw:
            pass
        qh, ql = sb("qh", [P, KT, S], FP32R), sb("ql", [P, KT, S], FP32R)
        kh, kl = sb("kh", [P, KT, S], FP32R), sb("kl", [P, KT, S], FP32R)
        wh, wl = sb("wh", [P, 5, 2048], FP32R), sb("wl", [P, 5, 2048], FP32R)
        decay = sb("decay", [P, RH, 384])
        rot = sb("rot", [P, TB, 2, 2, ROT])
        gn = sb("gn", [P, 2, KT])
        blk = sb("blk", [P, P])
        xn = sb("xn", [P, TB, C])
        st, mv = sb("st", [P, TB, 6]), sb("mv", [P, TB, 2])
        var, rstd, spare = sb("var", [P, TB]), sb("rstd", [P, TB]), sb("spare", [P, 1])
        two, power = sb("two", [P, 1]), sb("power", [P, 1])
        xh, xl = sb("xh", [P, KT, S], FP32R), sb("xl", [P, KT, S], FP32R)
        qk = sb("qk", [P, 2, TB, C])
        t1, t2 = (xn[:, t, 0:RH * ROT].rearrange("p (h d) -> p h d", h=RH) for t in range(TB))
        vraw = sb("vraw", [P, TB, C])
        vh, vl = sb("vh", [P, TB, RH, P], FP32R), sb("vl", [P, TB, RH, P], FP32R)
        graw = sb("graw", [P, KT, S])
        gc, u, n = (sb(k, [P, KT, S]) for k in ("gc", "u", "n"))
        sd = sb("sd", [P, 2, 384])
        sh, sl = sb("sh", [P, 2, 384], FP32R), sb("sl", [P, 2, 384], FP32R)
        gst, gmv = sb("gst", [P, KT, 6]), sb("gmv", [P, KT, 2])
        gsq, gm = sb("gsq", [P, KT, 1]), sb("gm", [P, KT, 2])
        gvar, ga, gb = sb("gvar", [P, KT]), sb("ga", [P, KT]), sb("gb", [P, KT])
        d, mish = u, n
        y, z = gc, u
        zh, zl = qh, ql

        def pb(name, shape):
            return mem.enter_context(nc.psum_tensor("a_" + name, shape, FP32))

        tp = pb("tp", [P, KT, S])
        gemm = pb("gemm", [P, 2, C])
        sc = pb("sc", [P, 2, 512])
        rt = pb("rt", [P, KT, S])

        x0_in, x_in = sem("x0_in"), sem("x_in")
        const_in = sem("const_in")
        raw_in = [sem("raw_in0"), sem("raw_in1")]
        wh_done, wl_done = sem("wh_done"), sem("wl_done")
        pads = sem("pads_zeroed")
        dve_own = sem("dve_own")
        var_done, rstd_done, gvar_done, gpow_done = sem("var_done"), sem("rstd_done"), sem("gvar_done"), sem("gpow_done")
        xn_done, tx_done, xh_done = sem("xn_done"), sem("tx_done"), sem("xh_done")
        xl_done = sem("xl_done")
        gemm_done, gemm_act = sem("gemm_done"), sem("gemm_act")
        rot_done, rot_added = sem("rot_done"), sem("rot_added")
        tq_done, tk_done, qh_done, kh_done = sem("tq_done"), sem("tk_done"), sem("qh_done"), sem("kh_done")
        ql_done, kl_done = sem("ql_done"), sem("kl_done")
        vh_done, vl_done = sem("vh_done"), sem("vl_done")
        sc_done, sd_done, sh_done, sl_done = sem("sc_done"), sem("sd_done"), sem("sh_done"), sem("sl_done")
        ret_done = sem("ret_done")
        gc_done, u_done, n_done, d_done, mish_done = (sem(k) for k in ("gc_done", "u_done", "n_done", "d_done", "mish_done"))
        gst_done, gmm_done, gmm_read, coef_done = sem("gst_done"), sem("gmm_done"), sem("gmm_read"), sem("coef_done")
        y_done, z_done, zh_done, zl_done = sem("y_done"), sem("z_done"), sem("zh_done"), sem("zl_done")
        wo_done, added = sem("wo_done"), sem("added")
        NPIECE = 5
        block = mem.enter_context(nc.Block())

        @block.sync
        def _(sp):
            sp.dma_start(X[:, 0:TB, :], x_dram[:, 0:TB, :]).then_inc(x0_in, 16)
            for k in range(NPIECE):
                if k >= 2:
                    sp.wait_ge(wl_done, k - 1)
                sp.dma_start(raw[:, k % 2, :], wa_dram[k, :, :]).then_inc(raw_in[k % 2], 16)
                if k == 1:
                    sp.dma_start(ident[:, :], ident_dram).then_inc(const_in, 16)
                    sp.dma_start(rot[:, :, :, :, :], rot_dram).then_inc(const_in, 16)
                    sp.dma_start(gn[:, :, :], gn_dram).then_inc(const_in, 16)
                    sp.dma_start(blk[:, :], blk_dram).then_inc(const_in, 16)
                    sp.dma_start(decay[:, :, :], decay_dram).then_inc(const_in, 16)
            sp.dma_start(X[:, TB:NT, :], x_dram[:, TB:NT, :]).then_inc(x_in, 16)

        @block.tensor
        def _(pe):
            def transpose_x(b, first):
                pe.wait_ge(xn_done, b + 1)
                if not first:
                    pe.wait_ge(ql_done, b)
                for t in range(TB):
                    for k in range(KT):
                        last = nc.tensor.transpose(tp[:, k, t * P:(t + 1) * P], xn[:, t, k * P:(k + 1) * P], ident[:, :])
                last.then_inc(tx_done, 1)

            def gemm_chunk(b, c, first):
                if not first or c >= 2:
                    if first:
                        pe.wait_ge(gemm_act, c - 1)
                        pe.wait_ge(rot_done, min(c - 1, 4))
                    else:
                        pe.wait_ge(gemm_act, b * 8 + (c - 1 if c >= 2 else 0))
                        pe.wait_ge(rot_done, b * 4 + (min(c - 1, 4) if c >= 2 else 0))
                        if c < 2:
                            pe.wait_ge(added, b * 2 - 1)
                bank = gemm[:, c % 2, :]
                if c < 6:
                    t, o = c % 2, (c // 2) * C
                    for k in range(KT):
                        if first and c == 0:
                            pe.wait_ge(wl_done, k + 1)
                        last = matmul3(nc, bank, (xh[:, k, t * P:(t + 1) * P], xl[:, k, t * P:(t + 1) * P]),
                                       (wh[:, k, o:o + C], wl[:, k, o:o + C]), k == 0, k == KT - 1)
                else:
                    for m in range(2):
                        o = 3 * C + (2 * (c - 6) + m) * P
                        for k in range(KT):
                            last = matmul3(nc, bank[:, m * S:(m + 1) * S], (wh[:, k, o:o + P], wl[:, k, o:o + P]),
                                           (xh[:, k, :], xl[:, k, :]), k == 0, k == KT - 1)
                last.then_inc(gemm_done, 1)

            def scores(b, h):
                pe.wait_ge(sd_done, b * 8 + h + 1)
                r, m = (h % 2) * RD, h // 2
                kk, qq = (kh[r:r + RD, m, :], kl[r:r + RD, m, :]), (qh[r:r + RD, m, :], ql[r:r + RD, m, :])
                matmul3(nc, sc[:, h % 2, 0:S], [a[:, 0:P] for a in kk], qq, True, True)
                matmul3(nc, sc[:, h % 2, S:384], [a[:, P:S] for a in kk], [a[:, P:S] for a in qq], True, True)\
                    .then_inc(sc_done, 1)

            def ret(b, h):
                pe.wait_ge(sh_done, b * 8 + h + 1)
                pe.wait_ge(sl_done, b * 8 + h + 3)
                m = h // 2
                first = h % 2 == 0
                matmul3(nc, rt[:, m, :], (vh[:, 0, h, :], vl[:, 0, h, :]), (sh[:, h % 2, 0:S], sl[:, h % 2, 0:S]), first, False)
                matmul3(nc, rt[:, m, P:S], (vh[:, 1, h, :], vl[:, 1, h, :]), (sh[:, h % 2, S:384], sl[:, h % 2, S:384]),
                        False, not first).then_inc(ret_done, 1)

            def body(b, nxt):
                pe.wait_ge(rot_added, b * 4 + 4)
                pe.wait_ge(gemm_act, b * 8 + 8)
                pe.wait_ge(xl_done, b + 1)
                pe.wait_ge(gmm_read, b + 1)
                for t in range(TB):
                    for k in range(KT):
                        last = nc.tensor.transpose(tp[:, k, t * P:(t + 1) * P], qk[:, 0, t, k * P:(k + 1) * P], ident[:, :])
                last.then_inc(tq_done, 1)
                pe.wait_ge(y_done, b + 1)
                for t in range(TB):
                    for k in range(KT):
                        last = nc.tensor.transpose(rt[:, k, t * P:(t + 1) * P], qk[:, 1, t, k * P:(k + 1) * P], ident[:, :])
                last.then_inc(tk_done, 1)
                if nxt:
                    transpose_x(b + 1, False)
                pe.wait_ge(ql_done, b + 1)
                pe.wait_ge(kl_done, b + 1)
                for h in range(RH):
                    scores(b, h)
                    if nxt:
                        if h == 0:
                            pe.wait_ge(xl_done, b + 2)
                        gemm_chunk(b + 1, h, False)
                    if h == 1:
                        pe.wait_ge(vh_done, b + 1)
                        pe.wait_ge(vl_done, b + 1)
                    if h >= 1:
                        ret(b, h - 1)
                ret(b, RH - 1)
                pe.wait_ge(gst_done, b + 1)
                nc.tensor.matmul(tp[:, 0, 0:2 * KT], blk[:, :], gm[:, :, :], start=True, stop=True).then_inc(gmm_done, 1)
                pe.wait_ge(zh_done, b + 1)
                pe.wait_ge(zl_done, b + 2)
                for t in range(TB):
                    if nxt:
                        pe.wait_ge(gemm_act, b * 8 + 15 + t)
                    else:
                        pe.wait_ge(added, b * 2 + 1)
                    for k in range(KT):
                        last = matmul3(nc, gemm[:, t, :], (zh[:, k, t * P:(t + 1) * P], zl[:, k, t * P:(t + 1) * P]),
                                       (wh[:, 4, k * C:(k + 1) * C], wl[:, 4, k * C:(k + 1) * C]), k == 0, k == KT - 1)
                    last.then_inc(wo_done, 1)

            pe.wait_ge(const_in, 80)
            transpose_x(0, True)
            pe.wait_ge(xl_done, 1)
            for c in range(8):
                gemm_chunk(0, c, True)
            pe.wait_ge(wl_done, NPIECE)
            with pe.Fori(0, B - 2) as b:
                body(b, True)
            body(B - 2, True)
            body(B - 1, False)

        @block.vector
        def _(dve):
            def layernorm(own, b):
                for t in range(TB):
                    tile = X[:, b * TB + t, :]
                    own.step(nc.vector.bn_stats(out=st[:, t, :], in_=tile))
                nc.vector.tensor_copy(spare[:, :], st[:, 0, 0:1])
                for t in range(TB):
                    last = nc.vector.bn_aggr(out=mv[:, t, :], in_=st[:, t, :])
                own.step(last)
                nc.vector.tensor_scalar(var[:, :], mv[:, :, 1], EPS, None, ALU.add).then_inc(var_done, 1)
                dve.wait_ge(rstd_done, b + 1)
                dve.wait_ge(tx_done, b)
                dve.wait_ge(rot_added, b * 4)
                for t in range(TB):
                    last = nc.vector.tensor_scalar(xn[:, t, :], X[:, b * TB + t, :], mv[:, t, 0:1], rstd[:, t:t + 1],
                                                   ALU.subtract, ALU.mult)
                last.then_inc(xn_done, 1)

            def x_low(b):
                dve.wait_ge(xh_done, b + 1)
                nc.vector.tensor_tensor(xl[:, :, :], tp[:, :, :], as_f32(xh[:, :, :]), ALU.subtract).then_inc(xl_done, 1)

            def rotate(c, gb, first=False):
                dve.wait_ge(gemm_act, gb * 8 + c + 1)
                if not first or c:
                    dve.wait_ge(rot_added, gb * 4 + c)
                t, which = c % 2, c // 2
                src = gemm[:, c % 2, :].rearrange("p (h d) -> p h d", h=RH)
                cos = rot[:, t, which, 0, :].rearrange("p (o d) -> p o d", o=1).to_broadcast([P, RH, ROT])
                sin = rot[:, t, which, 1, :].rearrange("p (o d) -> p o d", o=1).to_broadcast([P, RH, ROT])
                H = ROT // 2
                nc.vector.tensor_tensor(t1[:, :, :], src[:, :, 0:ROT], cos, ALU.mult)
                nc.vector.tensor_tensor(t2[:, :, 0:H], src[:, :, H:ROT], sin[:, :, 0:H], ALU.mult)
                nc.vector.tensor_tensor(t2[:, :, H:ROT], src[:, :, 0:H], sin[:, :, H:ROT], ALU.mult)\
                    .then_inc(rot_done, 1)

            OWN_PROLOGUE, OWN = 3, 15

            def body(b, nxt, norm, base):
                own = Chain(dve, dve_own, 0 if isinstance(b, int) else OWN, b, base)
                dve.wait_ge(qh_done, b + 1)
                nc.vector.tensor_tensor(ql[:, :, :], tp[:, :, :], as_f32(qh[:, :, :]), ALU.subtract).then_inc(ql_done, 1)
                dve.wait_ge(kh_done, b + 1)
                nc.vector.tensor_tensor(kl[:, :, :], rt[:, :, :], as_f32(kh[:, :, :]), ALU.subtract).then_inc(kl_done, 1)
                dve.wait_ge(gemm_act, b * 8 + 8)
                nc.vector.tensor_scalar(gc[:, :, :], graw[:, :, :], 20.0, None, ALU.min).then_inc(gc_done, 1)
                if nxt:
                    x_low(b + 1)
                for h in range(RH):
                    dve.wait_ge(sc_done, b * 8 + h + 1)
                    dve.wait_ge(sl_done, b * 8 + h + 1)
                    nc.vector.tensor_tensor(sd[:, h % 2, :], sc[:, h % 2, 0:384], decay[:, h, :], ALU.mult).then_inc(sd_done, 1)
                    if nxt and h < 4:
                        rotate(h, b + 1)
                    if h == 0:
                        dve.wait_ge(u_done, b + 1)
                        nc.vector.scalar_tensor_tensor(out=n[:, :, :], in0=u[:, :, :], scalar=2.0, in1=u[:, :, :],
                                                       op0=ALU.add, op1=ALU.mult).then_inc(n_done, 1)
                    if h == 1:
                        dve.wait_ge(d_done, b + 1)
                    if 1 <= h <= 4:
                        own.step(nc.vector.reciprocal(d[:, h - 1, :], d[:, h - 1, :]))
                    if h == 5:
                        own.step(nc.vector.tensor_tensor(n[:, :, :], n[:, :, :], d[:, :, :], ALU.mult))
                    if h == 6:
                        nc.vector.tensor_tensor(mish[:, :, :], n[:, :, :], graw[:, :, :], ALU.mult).then_inc(mish_done, 1)
                dve.wait_ge(ret_done, b * 8 + 10)
                for m in range(KT):
                    last = nc.vector.bn_stats(out=gst[:, m, :], in_=rt[:, m, :])
                own.step(last)
                nc.vector.tensor_copy(spare[:, :], gst[:, 0, 0:1])
                for m in range(KT):
                    last = nc.vector.bn_aggr(out=gmv[:, m, :], in_=gst[:, m, :])
                own.step(last)
                own.step(nc.vector.tensor_tensor(gsq[:, :, :], gmv[:, :, 0:1], gmv[:, :, 0:1], ALU.mult))
                nc.vector.tensor_copy(gm[:, :, 0:1], gmv[:, :, 0:1])
                nc.vector.tensor_tensor(gm[:, :, 1:2], gmv[:, :, 1:2], gsq[:, :, :], ALU.add).then_inc(gst_done, 1)
                dve.wait_ge(gmm_done, b + 1)
                nc.vector.tensor_copy(gmv[:, :, :], tp[:, 0, 0:2 * KT].rearrange("p (m s) -> p m s", s=2)).then_inc(gmm_read, 1)
                dve.wait_ge(gmm_read, b + 2)
                own.step(nc.vector.tensor_tensor(gsq[:, :, :], gmv[:, :, 0:1], gmv[:, :, 0:1], ALU.mult))
                own.step(nc.vector.tensor_tensor(gvar[:, :], gmv[:, :, 1], gsq[:, :, 0], ALU.subtract))
                nc.vector.tensor_scalar(gvar[:, :], gvar[:, :], EPS, None, ALU.add).then_inc(gvar_done, 1)
                dve.wait_ge(gpow_done, b + 1)
                own.step(nc.vector.tensor_tensor(ga[:, :], gvar[:, :], gn[:, 0, :], ALU.mult))
                own.step(nc.vector.tensor_tensor(gvar[:, :], gmv[:, :, 0], ga[:, :], ALU.mult))
                nc.vector.tensor_tensor(gb[:, :], gn[:, 1, :], gvar[:, :], ALU.subtract).then_inc(coef_done, 1)
                dve.wait_ge(y_done, b + 2)
                dve.wait_ge(mish_done, b + 1)
                nc.vector.tensor_tensor(z[:, :, :], y[:, :, :], mish[:, :, :], ALU.mult).then_inc(z_done, 1)
                if norm:
                    layernorm(own, b + 2)
                for t in range(TB):
                    dve.wait_ge(wo_done, b * 2 + t + 1)
                    tile = X[:, b * TB + t, :]
                    nc.vector.tensor_tensor(tile, tile, gemm[:, t, :], ALU.add).then_inc(added, 1)
                return base + own.n

            nc.vector.memset(gst[:, :, :], 0.0).then_inc(sd_done, 2)
            nc.vector.memset(gmv[:, :, :], 0.0).then_inc(gmm_read, 1)
            nc.vector.memset(gm[:, :, :], 0.0).then_inc(added, 1)
            own = Chain(dve, dve_own)
            dve.wait_ge(x0_in, 16)

            def first_norm(b):
                for t in range(TB):
                    tile = X[:, b * TB + t, :]
                    own.step(nc.vector.bn_stats(out=st[:, t, :], in_=tile))
                nc.vector.tensor_copy(spare[:, :], st[:, 0, 0:1])
                for t in range(TB):
                    last = nc.vector.bn_aggr(out=mv[:, t, :], in_=st[:, t, :])
                own.step(last)
                nc.vector.tensor_scalar(var[:, :], mv[:, :, 1], EPS, None, ALU.add).then_inc(var_done, 1)
                dve.wait_ge(rstd_done, b + 1)
                if b:
                    dve.wait_ge(tx_done, b)
                    dve.wait_ge(rot_added, b * 4)
                for t in range(TB):
                    last = nc.vector.tensor_scalar(xn[:, t, :], X[:, b * TB + t, :], mv[:, t, 0:1], rstd[:, t:t + 1],
                                                   ALU.subtract, ALU.mult)
                last.then_inc(xn_done, 1)

            first_norm(0)
            for k in range(NPIECE):
                dve.wait_ge(wh_done, k + 1)
                nc.vector.tensor_tensor(wl[:, k, :], raw[:, k % 2, :], as_f32(wh[:, k, :]), ALU.subtract).then_inc(wl_done, 1)
                if k == 1:
                    x_low(0)
            dve.wait_ge(const_in, 80)
            for c in range(4):
                rotate(c, 0, True)
            dve.wait_ge(x_in, 16)
            first_norm(1)
            assert own.n == OWN_PROLOGUE * 2
            with dve.Fori(0, B - 2) as b:
                steps = body(b, True, True, OWN_PROLOGUE * 2)
            assert steps == OWN_PROLOGUE * 2 + OWN, steps - OWN_PROLOGUE * 2
            steps = body(B - 2, True, False, OWN_PROLOGUE * 2 + (B - 2) * OWN)
            body(B - 1, False, False, steps)

        @block.scalar
        def _(act):
            def chunk_out(c, gb):
                act.wait_ge(gemm_done, gb * 8 + c + 1)
                bank = gemm[:, c % 2, :]
                if c < 4:
                    src = bank.rearrange("p (h d) -> p h d", h=RH)[:, :, ROT:RD]
                    dst = qk[:, c // 2, c % 2, :].rearrange("p (h d) -> p h d", h=RH)[:, :, ROT:RD]
                    nc.scalar.copy(dst, src).then_inc(gemm_act, 1)
                elif c < 6:
                    nc.scalar.copy(vraw[:, c - 4, :], bank).then_inc(gemm_act, 1)
                else:
                    g = 2 * (c - 6)
                    nc.scalar.copy(graw[:, g:g + 2, :].rearrange("p m s -> p (m s)"), bank).then_inc(gemm_act, 1)

            def body(b, nxt):
                act.wait_ge(tq_done, b + 1)
                nc.scalar.copy(qh[:, :, :], tp[:, :, :]).then_inc(qh_done, 1)
                act.wait_ge(tk_done, b + 1)
                nc.scalar.copy(kh[:, :, :], rt[:, :, :]).then_inc(kh_done, 1)
                if nxt:
                    act.wait_ge(tx_done, b + 2)
                    nc.scalar.copy(xh[:, :, :], tp[:, :, :]).then_inc(xh_done, 1)
                act.wait_ge(gemm_act, b * 8 + 8)
                act.wait_ge(ret_done, b * 8 + 2)
                for e in range(2):
                    dst = vh[:, :, :, e * RD:(e + 1) * RD].rearrange("p t (m e) d -> p t m e d", e=2)[:, :, :, e, :]
                    src = vraw[:, :, :].rearrange("p t (m e d) -> p t m e d", e=2, d=RD)[:, :, :, e, :]
                    last = nc.scalar.copy(dst, src)
                last.then_inc(vh_done, 1)
                act.wait_ge(gc_done, b + 1)
                act.wait_ge(zl_done, b + 1)
                nc.scalar.activation(u[:, :, :], gc[:, :, :], ACT.Exp).then_inc(u_done, 1)
                for h in range(RH):
                    act.wait_ge(sd_done, b * 8 + h + 3)
                    act.wait_ge(ret_done, b * 8 + h + 1)
                    nc.scalar.copy(sh[:, h % 2, :], sd[:, h % 2, :]).then_inc(sh_done, 1)
                    if nxt:
                        if h == 0:
                            act.wait_ge(tk_done, b + 1)
                        if h == 4:
                            act.wait_ge(vl_done, b + 1)
                        if h < 6:
                            chunk_out(h, b + 1)
                if nxt:
                    act.wait_ge(mish_done, b + 1)
                    chunk_out(6, b + 1)
                    chunk_out(7, b + 1)
                act.wait_ge(coef_done, b + 1)
                for m in range(KT):
                    last = nc.scalar.activation(y[:, m, :], rt[:, m, :], ACT.Identity, bias=gb[:, m:m + 1], scale=ga[:, m:m + 1])
                last.then_inc(y_done, 1)
                act.wait_ge(z_done, b + 1)
                nc.scalar.copy(zh[:, :, :], z[:, :, :]).then_inc(zh_done, 1)

            for k in range(NPIECE):
                act.wait_ge(raw_in[k % 2], 16 * (k // 2 + 1))
                nc.scalar.copy(wh[:, k, :], raw[:, k % 2, :]).then_inc(wh_done, 1)
                if k == 1:
                    act.wait_ge(tx_done, 1)
                    nc.scalar.copy(xh[:, :, :], tp[:, :, :]).then_inc(xh_done, 1)
            for c in range(8):
                chunk_out(c, 0)
            act.wait_ge(wl_done, NPIECE)
            with act.Fori(0, B - 2) as b:
                body(b, True)
            body(B - 2, True)
            body(B - 1, False)

        @block.gpsimd
        def _(pool):
            def flat(a):
                return a[:, :, :].rearrange("p m s -> p (m s)")

            def root(b):
                pool.wait_ge(var_done, b + 1)
                nc.gpsimd.tensor_tensor(rstd[:, :], var[:, :], power[:, :].to_broadcast([P, TB]), ALU.pow).then_inc(rstd_done, 1)

            def rotated(c, gb):
                pool.wait_ge(rot_done, gb * 4 + c + 1)
                dst = qk[:, c // 2, c % 2, :].rearrange("p (h d) -> p h d", h=RH)[:, :, 0:ROT]
                nc.gpsimd.tensor_tensor(dst, t1[:, :, :], t2[:, :, :], ALU.add).then_inc(rot_added, 1)

            def body(b, nxt, norm):
                pool.wait_ge(vh_done, b + 1)
                for e in range(2):
                    dst, hi = (a[:, :, :, e * RD:(e + 1) * RD].rearrange("p t (m e) d -> p t m e d", e=2)[:, :, :, e, :] for a in (vl, vh))
                    src = vraw[:, :, :].rearrange("p t (m e d) -> p t m e d", e=2, d=RD)[:, :, :, e, :]
                    last = nc.gpsimd.tensor_tensor(dst, src, as_f32(hi), ALU.subtract)
                last.then_inc(vl_done, 1)
                for h in range(RH):
                    pool.wait_ge(sh_done, b * 8 + h + 1)
                    nc.gpsimd.tensor_tensor(sl[:, h % 2, :], sd[:, h % 2, :], as_f32(sh[:, h % 2, :]), ALU.subtract).then_inc(sl_done, 1)
                    if h == 0:
                        pool.wait_ge(n_done, b + 1)
                        nc.gpsimd.tensor_tensor(flat(d), flat(n), two[:, :].to_broadcast([P, KT * S]), ALU.add).then_inc(d_done, 1)
                        if nxt:
                            pool.wait_ge(tk_done, b + 1)
                    if nxt and h < 4:
                        rotated(h, b + 1)
                pool.wait_ge(gvar_done, b + 1)
                nc.gpsimd.tensor_tensor(gvar[:, :], gvar[:, :], power[:, :].to_broadcast([P, KT]), ALU.pow).then_inc(gpow_done, 1)
                pool.wait_ge(zh_done, b + 1)
                nc.gpsimd.tensor_tensor(zl[:, :, :], z[:, :, :], as_f32(zh[:, :, :]), ALU.subtract).then_inc(zl_done, 1)
                if norm:
                    root(b + 2)

            nc.gpsimd.memset(as_f32(vh[:, :, :, :]), 0.0).then_inc(pads, 1)
            nc.gpsimd.memset(as_f32(vl[:, :, :, :]), 0.0).then_inc(pads, 1)
            for a, value in ((two, 2.0), (power, -0.5)):
                nc.gpsimd.memset(a[:, :], value).then_inc(pads, 1)
            pool.wait_ge(pads, 4)
            pool.sem_inc(zl_done, 1)
            pool.sem_inc(sl_done, 2)
            pool.sem_inc(ret_done, 2)
            pool.sem_inc(y_done, 1)
            root(0)
            for c in range(4):
                rotated(c, 0)
            root(1)
            with pool.Fori(0, B - 2) as b:
                body(b, True, True)
            body(B - 2, True, False)
            body(B - 1, False, False)


def cross_attention(nc, X, wb_dram, ctx_dram, pos_dram, freq_dram, bout_dram, ident):
    HB = 2 * 64
    TWO_PI = 2.0 * np.pi
    with ExitStack() as mem:
        def sb(name, shape, dt=FP32):
            return mem.enter_context(nc.sbuf_tensor("b_" + name, shape, dt))

        def sem(name):
            return nc.alloc_semaphore("b_" + name)

        wh, wl = sb("wh", [P, 3, 2048], FP32R), sb("wl", [P, 3, 2048], FP32R)
        qs = sb("qs", [P, 2, TB, XH * 64])
        qT, kT = sb("qT", [P, XH // 2, S], FP32R), sb("kT", [P, XH // 2, S], FP32R)
        xn = sb("xn", [P, TB, C])
        xh, xl = sb("xh", [P, KT, S], FP32R), sb("xl", [P, KT, S], FP32R)
        craw = sb("craw", [P, CKT, S])
        ch, cl = sb("ch", [P, CKT, S], FP32R), sb("cl", [P, CKT, S], FP32R)
        pr = sb("pr", [P, 4, TB, S])
        vn, v1 = sb("vn", [P, TB, XH, XD]), sb("v1", [P, TB, XH, XD + 1])
        attn = sb("attn", [P, TB, C])
        ah, al = xh, xl
        ac, bs = sb("ac", [P, 2, XH, 8]), sb("bs", [P, 2, XH, 8])
        rr = sb("rr", [P, XH, XD])
        pos, freq, bout = sb("pos", [P, NT, 2]), sb("freq", [P, 2, 4]), sb("bout", [P, C])
        ang, turns, cs = (sb(k, [P, 2, NT * 8]) for k in ("ang", "turns", "cs"))
        st, mv = sb("st", [P, TB, 6]), sb("mv", [P, TB, 2])
        var, rstd, spare, power = sb("var", [P, TB]), sb("rstd", [P, TB]), sb("spare", [P, 1]), sb("power", [P, 1])
        zero = sb("zero", [P, 1])
        mx = sb("mx", [P, TB, XH])
        nm = sb("nm", [P, TB, P])
        mT = sb("mT", [32, 2, S], FP32R)
        rs = sb("rs", [P, TB, 8])

        def pb(name, shape):
            return mem.enter_context(nc.psum_tensor("b_" + name, shape, FP32))

        rt = pb("rt", [P, 4, 512])
        av = pb("av", [P, 2, 512])
        gm = pb("gm", [P, 2, 512])

        raw_in, pos_in, ctx_in = sem("raw_in"), sem("pos_in"), sem("ctx_in")
        presets, own_sem = sem("presets"), sem("dve_own")
        wh_done, wl_done = sem("wh_done"), sem("wl_done")
        ang_done, cs_done = sem("ang_done"), sem("cs_done")
        var_done, rstd_done, xn_done = sem("var_done"), sem("rstd_done"), sem("xn_done")
        ch_done, cl_done = sem("ch_done"), sem("cl_done")
        gm_mm, gm_read = [sem("gm_mm0"), sem("gm_mm1")], [sem("gm_read0"), sem("gm_read1")]
        xh_done = sem("xh_done")
        summed, rh_done, rl_done = sem("summed"), sem("rh_done"), sem("rl_done")
        vn_done, v1_done = sem("vn_done"), sem("v1_done")
        tq_mm, tq_act, tq_dve = sem("tq_mm"), sem("tq_act"), sem("tq_dve")
        row_mm, mx_done, nm_done = sem("row_mm"), sem("mx_done"), sem("nm_done")
        nmh_done = sem("nmh_done")
        m_moved = [sem("m_moved0"), sem("m_moved1")]
        st_mm, e_done, av_done, rs_done, attn_done = (sem(k) for k in ("st_mm", "e_done", "av_done", "rs_done", "attn_done"))
        ah_done = sem("ah_done")
        LAGS, LAGV = 20, 22
        PIECE = {2: 2, 4: 3, 6: 4, 8: 5, 10: 6, 12: 7}
        block = mem.enter_context(nc.Block())

        def index(b, u, nxt=True):
            return b * 7 + (4 + (u if nxt else u - 8) // 2)

        @block.sync
        def _(sp):
            sp.dma_start(pos[:, :, :], pos_dram).then_inc(pos_in, 16)
            sp.dma_start(freq[:, :, :], freq_dram).then_inc(pos_in, 16)
            sp.dma_start(bout[:, :], bout_dram).then_inc(pos_in, 16)
            sp.dma_start(craw[:, :, :], ctx_dram[0, :, :, :]).then_inc(ctx_in, 16)
            for k in range(3):
                sp.dma_start(qs[:, k // 2, k % 2, :], wb_dram[k, :, :]).then_inc(raw_in, 16)

            def body(b, nxt):
                if nxt:
                    sp.wait_ge(cl_done, b + 1)
                    sp.dma_start(craw[:, :, :], ctx_dram[b + 1, :, :, :]).then_inc(ctx_in, 16)
                for k in range(2):
                    sp.wait_ge(gm_read[k], index(b, 8 + k, nxt) + 1)
                    for c in range(2):
                        for e in range(2):
                            row = 64 * e + 48 + c
                            sp.dma_start(as_f32(qT[row:row + 1, 8 * k:8 * k + 8, :]),
                                         as_f32(mT[16 * c + e:16 * c + e + 15:2, k, :])).then_inc(m_moved[k], 16)

            with sp.Fori(0, B - 1) as b:
                body(b, True)
            body(B - 1, False)

        @block.tensor
        def _(pe):
            def take(b, u, nxt=True):
                pe.wait_ge(gm_read[u % 2], index(b, u, nxt))
                return gm[:, u % 2, :]

            def transpose_x(b, t):
                bank = gm[:, t, :]
                for m in range(KT):
                    last = nc.tensor.transpose(bank[:, m * P:(m + 1) * P], xn[:, t, m * P:(m + 1) * P], ident[:, :])
                last.then_inc(gm_mm[t], 1)

            def product(u):
                t, bank = u % 2, gm[:, u % 2, :]
                a = slice(t * P, (t + 1) * P)
                if u < 4:
                    for m in range(KT):
                        last = matmul3(nc, bank, (xh[:, m, a], xl[:, m, a]), (wh[:, 0, m * C:(m + 1) * C], wl[:, 0, m * C:(m + 1) * C]),
                                       m == 0, m == KT - 1)
                else:
                    for m in range(CKT):
                        o = m * 2 * C + (u // 2 - 2) * C
                        last = matmul3(nc, bank, (ch[:, m, a], cl[:, m, a]), (wh[:, 1, o:o + C], wl[:, 1, o:o + C]),
                                       m == 0, m == CKT - 1)
                last.then_inc(gm_mm[t], 1)

            def transpose_qk(gb, first):
                pe.wait_ge(rl_done, gb * 4 + 4)
                for j in range(16):
                    which, t, four = j // 8, (j // 4) % 2, j % 4
                    if j >= 4:
                        pe.wait_ge((tq_act, tq_dve)[j % 2], gb * 8 + ((j - 4) // 2 + 1))
                    for m in range(4):
                        c = (four * 4 + m) * P
                        last = nc.tensor.transpose(rt[:, j % 4, m * P:(m + 1) * P], qs[:, which, t, c:c + P], ident[:, :])
                    last.then_inc(tq_mm, 1)

            def rows(b, h):
                pe.wait_ge(mx_done, b * XH + (h + 1))
                r, m = 64 * (h % 2), h // 2
                for t in range(TB):
                    last = nc.tensor.matmul(rt[:, h % 2, t * S:(t + 1) * S], qT[r:r + 64, m, t * P:(t + 1) * P], kT[r:r + 64, m, :],
                                            start=True, stop=True)
                last.then_inc(row_mm, 1)

            def logits(b, h):
                if h % 16 == 0:
                    pe.wait_ge(m_moved[h // 16], b * 64 + 64)
                pe.wait_ge(e_done, b * XH + (h + 1))
                r, m = 64 * (h % 2), h // 2
                for j in range(TB):
                    last = nc.tensor.matmul(rt[:, 2 + h % 2, j * S:(j + 1) * S], kT[r:r + 64, m, j * P:(j + 1) * P], qT[r:r + 64, m, :],
                                            start=True, stop=True)
                last.then_inc(st_mm, 1)

            def values(b, h):
                g = h // 8
                if h == 0:
                    pe.wait_ge(v1_done, b + 1)
                if h % 8 == 0:
                    pe.wait_ge(attn_done, b * 4 + (g + 1))
                pe.wait_ge(e_done, b * XH + (h + 3))
                for t in range(TB):
                    o = (t * 8 + h % 8) * (XD + 1)
                    for j in range(TB):
                        last = nc.tensor.matmul(av[:, g % 2, o:o + XD + 1], pr[:, h % 4, j, t * P:(t + 1) * P], v1[:, j, h, :],
                                                start=j == 0, stop=j == TB - 1)
                last.then_inc(av_done, 1)

            def body(b, nxt):
                pe.wait_ge(tq_act, b * 8 + 8)
                pe.wait_ge(tq_dve, b * 8 + 8)
                for i in range(XH + LAGV):
                    if i < XH:
                        rows(b, i)
                    if i == 1 and nxt:
                        pe.wait_ge(xn_done, b + 2)
                        for t in range(TB):
                            take(b, t)
                            transpose_x(b + 1, t)
                    if i in PIECE and nxt:
                        u = PIECE[i]
                        if u == 4:
                            pe.wait_ge(cl_done, b + 2)
                        take(b, u)
                        product(u)
                    if i in (18, 34):
                        k = i // 32
                        pe.wait_ge(nm_done, b * 2 + (k + 1))
                        bank = take(b, 8 + k, nxt)
                        for t in range(TB):
                            last = nc.tensor.transpose(bank[:, t * P:(t + 1) * P], nm[:, t, :], ident[:, :])
                        last.then_inc(gm_mm[k], 1)
                    if LAGS <= i < LAGS + XH:
                        logits(b, i - LAGS)
                    if i >= LAGV:
                        values(b, i - LAGV)
                if nxt:
                    pe.wait_ge(e_done, b * XH + (XH + 2))
                    transpose_qk(b + 1, False)
                pe.wait_ge(attn_done, b * 4 + 6)
                for t in range(TB):
                    bank = take(b, 10 + t, nxt)
                    for m in range(KT):
                        last = nc.tensor.transpose(bank[:, m * P:(m + 1) * P], attn[:, t, m * P:(m + 1) * P], ident[:, :])
                    last.then_inc(gm_mm[t], 1)
                for t in range(TB):
                    bank = take(b, 12 + t, nxt)
                    a = slice(t * P, (t + 1) * P)
                    for m in range(KT):
                        last = matmul3(nc, bank, (ah[:, m, a], al[:, m, a]), (wh[:, 2, m * C:(m + 1) * C], wl[:, 2, m * C:(m + 1) * C]),
                                       m == 0, m == KT - 1)
                    last.then_inc(gm_mm[t], 1)

            pe.wait_ge(xn_done, 1)
            for t in range(TB):
                transpose_x(0, t)
            pe.wait_ge(wl_done, 3)
            pe.wait_ge(cl_done, 1)
            for u in range(2, 8):
                pe.wait_ge(gm_read[u % 2], u // 2)
                product(u)
            transpose_qk(0, True)
            with pe.Fori(0, B - 2) as b:
                body(b, True)
            body(B - 2, True)
            body(B - 1, False)

        @block.vector
        def _(dve):
            def statistics(own, b):
                for t in range(TB):
                    last = nc.vector.bn_stats(out=st[:, t, :], in_=X[:, b * TB + t, :])
                own.step(last)
                nc.vector.tensor_copy(spare[:, :], st[:, 0, 0:1])
                for t in range(TB):
                    last = nc.vector.bn_aggr(out=mv[:, t, :], in_=st[:, t, :])
                own.step(last)
                nc.vector.tensor_scalar(var[:, :], mv[:, :, 1], EPS, None, ALU.add).then_inc(var_done, 1)
                dve.wait_ge(rstd_done, b + 1)
                for t in range(TB):
                    last = nc.vector.tensor_scalar(xn[:, t, :], X[:, b * TB + t, :], mv[:, t, 0:1], rstd[:, t:t + 1],
                                                   ALU.subtract, ALU.mult)
                last.then_inc(xn_done, 1)

            def split_x(gb, t):
                a = slice(t * P, (t + 1) * P)
                dve.wait_ge(xh_done, gb * 2 + (t + 1))
                nc.vector.tensor_tensor(xl[:, :, a], gm[:, t, :].rearrange("p (m s) -> p m s", s=P), as_f32(xh[:, :, a]), ALU.subtract)\
                    .then_inc(gm_read[t], 1)

            def turn(gb, u, mm):
                t = u % 2
                dve.wait_ge(gm_mm[t], mm)
                if not (isinstance(gb, int) and gb == 0 and u == 2):
                    dve.wait_ge(summed, gb * 4 + (u - 2))
                src = gm[:, t, :].rearrange("p (k i) -> p k i", i=8)
                for k, dst in enumerate((ac, bs)):
                    table = cs[:, k, bass.ts(gb * TB + t, 8)].rearrange("p (o i) -> p o i", o=1).to_broadcast([P, 2 * XH, 8])
                    last = nc.vector.tensor_tensor(dst[:, :, :, :].rearrange("p c h i -> p (c h) i"), src, table, ALU.mult)
                last.then_inc(gm_read[t], 1)

            def group(b, g):
                dve.wait_ge(attn_done, b * 4 + (g + 2))
                dve.wait_ge(av_done, b * XH + (8 * g + 12))
                src = av[:, g % 2, 0:TB * 8 * (XD + 1)].rearrange("p (t h d) -> p t h d", t=TB, h=8)
                nc.vector.reciprocal(rs[:, :, :], src[:, :, :, XD]).then_inc(rs_done, 1)
                dve.wait_ge(rs_done, b * 4 + (g + 1))
                dst = attn[:, :, g * P:(g + 1) * P].rearrange("p t (h d) -> p t h d", h=8)
                for t in range(TB):
                    last = nc.vector.tensor_tensor(dst[:, t], src[:, t, :, 0:XD],
                                                   rs[:, t, :].rearrange("p (h o) -> p h o", o=1).to_broadcast([P, 8, XD]), ALU.mult)
                last.then_inc(attn_done, 1)

            OWN = 3

            def body(b, nxt, norm, base):
                own = Chain(dve, own_sem, 0 if isinstance(b, int) else OWN, b, base)
                for i in range(XH + LAGV):
                    if i < XH:
                        dve.wait_ge(row_mm, b * XH + (i + 1))
                        nc.vector.tensor_reduce(out=mx[:, :, i], in_=rt[:, i % 2, :].rearrange("p (t s) -> p t s", s=S),
                                                op=ALU.max, axis=AX.X).then_inc(mx_done, 1)
                    if i == 1 and nxt:
                        for t in range(TB):
                            split_x(b + 1, t)
                    if i - 1 in PIECE and PIECE[i - 1] < 6 and nxt:
                        turn(b + 1, PIECE[i - 1], index(b, PIECE[i - 1]) + 1)
                    if i in (15, 31):
                        k = i // 16
                        dve.wait_ge(mx_done, b * XH + (i + 3))
                        part = mx[:, :, 16 * k:16 * k + 16]
                        if k:
                            dve.wait_ge(gm_read[0], index(b, 8, nxt) + 1)
                        nc.vector.tensor_scalar(nm[:, :, 0:16].bitcast(FP32R), part, -1.0, None, ALU.mult).then_inc(nmh_done, 1)
                        dve.wait_ge(nmh_done, b * 2 + (k + 1))
                        nc.vector.scalar_tensor_tensor(out=nm[:, :, 16:32], in0=part, scalar=-1.0, in1=nm[:, :, 0:16],
                                                       op0=ALU.mult, op1=ALU.subtract).then_inc(nm_done, 1)
                    if i >= 32 and (i - 32) % 8 == 0 and (i - 32) // 8 < 3:
                        group(b, (i - 32) // 8)
                group(b, 3)
                if nxt:
                    columns(b + 1)
                for t in range(TB):
                    a = slice(t * P, (t + 1) * P)
                    dve.wait_ge(ah_done, b * 2 + (t + 1))
                    nc.vector.tensor_tensor(al[:, :, a], gm[:, t, :].rearrange("p (m s) -> p m s", s=P), as_f32(ah[:, :, a]), ALU.subtract)\
                        .then_inc(gm_read[t], 1)
                if norm:
                    statistics(own, b + 2)
                for t in range(TB):
                    dve.wait_ge(gm_mm[t], index(b, 12 + t, nxt) + 1)
                    tile = X[:, b * TB + t, :]
                    nc.vector.tensor_tensor(attn[:, t, :], gm[:, t, :], bout[:, :], ALU.add).then_inc(gm_read[t], 1)
                    dve.wait_ge(gm_read[t], index(b, 12 + t, nxt) + 1)
                    last = nc.vector.tensor_tensor(tile, tile, attn[:, t, :], ALU.add)
                own.step(last)
                return base + own.n

            def columns(gb):
                for j in range(1, 16, 2):
                    dve.wait_ge(tq_mm, gb * 16 + (j + 1))
                    which, t, four = j // 8, (j // 4) % 2, j % 4
                    nc.vector.tensor_copy((qT, kT)[which][:, four * 4:four * 4 + 4, t * P:(t + 1) * P],
                                          rt[:, j % 4, :].rearrange("p (m s) -> p m s", s=P)).then_inc(tq_dve, 1)

            own = Chain(dve, own_sem)
            statistics(own, 0)
            dve.wait_ge(pos_in, 48)
            an = ang[:, 1, :].rearrange("p (t a i) -> p t a i", a=2, i=4)
            fr = freq[:, :, :].rearrange("p (o a) i -> p o a i", o=1).to_broadcast([P, NT, 2, 4])
            ps = pos[:, :, :].rearrange("p t (a o) -> p t a o", o=1).to_broadcast([P, NT, 2, 4])
            own.step(nc.vector.tensor_tensor(an, ps, fr, ALU.mult))
            own.step(nc.vector.tensor_scalar(ang[:, 0, :], ang[:, 1, :], float(np.pi / 2), None, ALU.add))
            ROUND = 1.5 * 2.0 ** 23
            own.step(nc.vector.tensor_scalar(turns[:, :, :], ang[:, :, :], 1.0 / TWO_PI, ROUND, ALU.mult, ALU.add))
            own.step(nc.vector.tensor_scalar(turns[:, :, :], turns[:, :, :], -ROUND, None, ALU.add))
            for part in (6.28125, TWO_PI - 6.28125):
                own.step(nc.vector.scalar_tensor_tensor(out=ang[:, :, :], in0=turns[:, :, :], scalar=-part, in1=ang[:, :, :],
                                                        op0=ALU.mult, op1=ALU.add))
            nc.vector.tensor_scalar(ang[:, :, :], ang[:, :, :], 3.1415925, -3.1415925, ALU.min, ALU.max).then_inc(ang_done, 1)
            dve.sem_inc(mx_done, 2)
            for k in range(3):
                dve.wait_ge(wh_done, k + 1)
                nc.vector.tensor_tensor(wl[:, k, :], qs[:, k // 2, k % 2, :], as_f32(wh[:, k, :]), ALU.subtract).then_inc(wl_done, 1)
            for t in range(TB):
                split_x(0, t)
            dve.wait_ge(cs_done, 1)
            for u in range(2, 6):
                turn(0, u, u // 2 + 1)
            columns(0)
            statistics(own, 1)
            base = own.n
            with dve.Fori(0, B - 2) as b:
                steps = body(b, True, True, base)
            assert steps == base + OWN, steps - base
            steps = body(B - 2, True, False, base + (B - 2) * OWN)
            body(B - 1, False, False, steps)

        @block.scalar
        def _(act):
            def high_x(gb, t, mm):
                a = slice(t * P, (t + 1) * P)
                act.wait_ge(gm_mm[t], mm)
                nc.scalar.copy(xh[:, :, a], gm[:, t, :].rearrange("p (m s) -> p m s", s=P)).then_inc(xh_done, 1)

            def high_context(gb):
                act.wait_ge(ctx_in, gb * 16 + 16)
                nc.scalar.copy(ch[:, :, :], craw[:, :, :]).then_inc(ch_done, 1)

            def high_rows(gb, u):
                act.wait_ge(summed, gb * 4 + (u - 1))
                which, t = u // 2 - 1, u % 2
                apart = 32 if which == 0 else 16
                head = qs[:, which, t, :].rearrange("p (h d) -> p h d", h=XH)
                for k in range(2):
                    last = nc.scalar.copy(head[:, :, k * apart:k * apart + XD].bitcast(FP32R), rr[:, :, :])
                last.then_inc(rh_done, 1)

            def v_out(gb, t, mm):
                act.wait_ge(gm_mm[t], mm)
                nc.scalar.copy(vn[:, t, :, :].rearrange("p h d -> p (h d)"), gm[:, t, :]).then_inc(gm_read[t], 1)

            def columns(gb):
                for j in range(0, 16, 2):
                    act.wait_ge(tq_mm, gb * 16 + (j + 1))
                    which, t, four = j // 8, (j // 4) % 2, j % 4
                    nc.scalar.copy((qT, kT)[which][:, four * 4:four * 4 + 4, t * P:(t + 1) * P],
                                   rt[:, j % 4, :].rearrange("p (m s) -> p m s", s=P)).then_inc(tq_act, 1)

            def body(b, nxt):
                for i in range(XH + LAGV):
                    if nxt:
                        if i == 0:
                            high_context(b + 1)
                        if i == 1:
                            for t in range(TB):
                                high_x(b + 1, t, index(b, t) + 1)
                        if i - 1 in PIECE:
                            u = PIECE[i - 1]
                            if u < 6:
                                high_rows(b + 1, u)
                            else:
                                if u == 6:
                                    act.wait_ge(v1_done, b + 1)
                                v_out(b + 1, u % 2, index(b, u) + 1)
                    if i in (18, 34):
                        k = i // 32
                        act.wait_ge(gm_mm[k], index(b, 8 + k, nxt) + 1)
                        nc.scalar.copy(mT[:, k, :], gm[0:32, k, 0:S]).then_inc(gm_read[k], 1)
                    if LAGS <= i < LAGS + XH:
                        h = i - LAGS
                        act.wait_ge(st_mm, b * XH + (h + 1))
                        act.wait_ge(av_done, b * XH + (h + 1))
                        nc.scalar.activation(pr[:, h % 4, :, :].rearrange("p j s -> p (j s)"), rt[:, 2 + h % 2, :], ACT.Exp,
                                             scale=XD ** -0.5).then_inc(e_done, 1)
                if nxt:
                    columns(b + 1)
                for t in range(TB):
                    a = slice(t * P, (t + 1) * P)
                    act.wait_ge(gm_mm[t], index(b, 10 + t, nxt) + 1)
                    nc.scalar.copy(ah[:, :, a], gm[:, t, :].rearrange("p (m s) -> p m s", s=P)).then_inc(ah_done, 1)

            act.wait_ge(raw_in, 48)
            for k in range(3):
                nc.scalar.copy(wh[:, k, :], qs[:, k // 2, k % 2, :]).then_inc(wh_done, 1)
            for t in range(TB):
                high_x(0, t, 1)
            high_context(0)
            act.wait_ge(ang_done, 1)
            nc.scalar.activation(cs[:, :, :], ang[:, :, :], ACT.Sin).then_inc(cs_done, 1)
            act.wait_ge(presets, 7)
            for u in range(2, 6):
                high_rows(0, u)
            for t in range(TB):
                v_out(0, t, 4)
            columns(0)
            with act.Fori(0, B - 2) as b:
                body(b, True)
            body(B - 2, True)
            body(B - 1, False)

        @block.gpsimd
        def _(pool):
            def root(b):
                pool.wait_ge(var_done, b + 1)
                nc.gpsimd.tensor_tensor(rstd[:, :], var[:, :], power[:, :].to_broadcast([P, TB]), ALU.pow).then_inc(rstd_done, 1)

            def low_context(gb):
                pool.wait_ge(ch_done, gb + 1)
                nc.gpsimd.tensor_tensor(cl[:, :, :], craw[:, :, :], as_f32(ch[:, :, :]), ALU.subtract).then_inc(cl_done, 1)

            def low_rows(gb, u, mm):
                pool.wait_ge(gm_read[u % 2], mm)
                if not (isinstance(gb, int) and gb * 4 + u == 2):
                    pool.wait_ge(rl_done, gb * 4 + (u - 2))
                which, t = u // 2 - 1, u % 2
                nc.gpsimd.tensor_tensor(rr[:, :, 0:8], ac[:, 0, :, :], bs[:, 1, :, :], ALU.subtract)
                nc.gpsimd.tensor_tensor(rr[:, :, 8:16], bs[:, 0, :, :], ac[:, 1, :, :], ALU.add).then_inc(summed, 1)
                pool.wait_ge(rh_done, gb * 4 + (u - 1))
                o = 16 if which == 0 else 32
                head = qs[:, which, t, :].rearrange("p (h d) -> p h d", h=XH)
                nc.gpsimd.tensor_tensor(head[:, :, o:o + XD], rr[:, :, :], head[:, :, 0:XD], ALU.subtract).then_inc(rl_done, 1)

            def v_in(gb, mm):
                for t in range(TB):
                    pool.wait_ge(gm_read[t], mm)
                pool.wait_ge(av_done, gb * XH + 4)
                for t in range(TB):
                    last = nc.gpsimd.tensor_tensor(v1[:, t, :, 0:XD], vn[:, t, :, :],
                                                   zero[:, :].rearrange("p (a o) -> p a o", o=1).to_broadcast([P, XH, XD]), ALU.add)
                last.then_inc(v1_done, 1)

            def body(b, nxt, norm):
                if nxt:
                    low_context(b + 1)
                    for u in range(2, 6):
                        low_rows(b + 1, u, index(b, u) + 1)
                    v_in(b + 1, index(b, 6) + 1)
                if norm:
                    root(b + 2)

            nc.gpsimd.memset(power[:, :], -0.5).then_inc(presets, 1)
            nc.gpsimd.memset(zero[:, :], 0.0).then_inc(presets, 1)
            nc.gpsimd.memset(v1[:, :, :, :], 1.0).then_inc(presets, 1)
            nc.gpsimd.memset(nm[:, :, :], 0.0).then_inc(presets, 1)
            pool.wait_ge(presets, 4)
            pool.sem_inc(e_done, 2)
            pool.sem_inc(av_done, 4)
            pool.sem_inc(attn_done, 2)
            root(0)
            low_context(0)
            pool.wait_ge(wl_done, 3)
            nc.gpsimd.memset(qs[:, 0, :, :], 0.0).then_inc(presets, 1)
            nc.gpsimd.memset(qs[:, 1, :, :], 0.0).then_inc(presets, 1)
            pool.wait_ge(presets, 6)
            nc.gpsimd.memset(qs[:, 1, :, :].rearrange("p t (h d) -> p (t h) d", d=64)[:, :, 48:50], 1.0).then_inc(presets, 1)
            pool.wait_ge(presets, 7)
            for u in range(2, 6):
                low_rows(0, u, u // 2 + 1)
            v_in(0, 4)
            root(1)
            with pool.Fori(0, B - 2) as b:
                body(b, True, True)
            body(B - 2, True, False)
            body(B - 1, False, False)


def feed_forward(nc, X, wc_dram, sel_dram, gate_dram, key_dram, ident, out_dram):
    G = NT // 4
    PW = 3 * C
    with ExitStack() as mem:
        def sb(name, shape, dt=FP32):
            return mem.enter_context(nc.sbuf_tensor("c_" + name, shape, dt))

        def pb(name, shape, stack):
            return stack.enter_context(nc.psum_tensor("c_" + name, shape, FP32))

        def sem(name):
            return nc.alloc_semaphore("c_" + name)

        xh, xl = sb("xh", [P, KT, NT * P], FP32R), sb("xl", [P, KT, NT * P], FP32R)
        raw, sraw = sb("raw", [P, 2, PW]), sb("sraw", [32, 2, P])
        wh, wl = sb("wh", [P, 4, PW], FP32R), sb("wl", [P, 4, PW], FP32R)
        sel = sb("sel", [32, 4, P], FP32R)
        cT = sb("cT", [32, NT * P], FP32R)
        with nc.sbuf_tensor("c_xn", [P, 4, C], FP32) as xn:
            pass
        with nc.sbuf_tensor("c_cc", [P, NT, P], FP32) as cc:
            pass
        hh = sb("hh", [P, 4, C], FP32R)
        hl = sb("hl", [P, 4, C], FP32R)
        s, t, hf = sb("s", [P, 2, C]), sb("t", [P, C]), sb("hf", [P, 2, C])
        st, mv = sb("st", [P, 4, 6]), sb("mv", [P, 4, 2])
        var, rstd, spare, power = sb("var", [P, 4]), sb("rstd", [P, 4]), sb("spare", [P, 1]), sb("power", [P, 1])
        zero = sb("zero", [P, 1])
        graw = sb("graw", [P, KT, P])
        gwh, gwl = sb("gwh", [P, KT, P], FP32R), sb("gwl", [P, KT, P], FP32R)
        lg = sb("lg", [P, C])
        L = sb("L", [P, NT, 16])
        key = sb("key", [P, E])
        prob, work, chosen, hit = (sb(k, [P, NT, E]) for k in ("prob", "work", "chosen", "hit"))
        top, den = sb("top", [P, NT]), sb("den", [P, NT])
        shared = sb("shared", [P, NT])

        with ExitStack() as early:
            tp = pb("tp", [P, 4, C], early)
            rl, rt = pb("rl", [P, C], early), pb("rt", [P, 4, P], early)
        fc = pb("fc", [P, 2, 2, C], mem)
        gate = pb("gate", [P, C], mem)
        yp = pb("yp", [P, 3, C], mem)

        raw_in, sraw_in = [sem("raw_in0"), sem("raw_in1")], [sem("sraw_in0"), sem("sraw_in1")]
        const_in, out_done = sem("const_in"), sem("out_done")
        own_sem = sem("dve_own")
        var_done, rstd_done, xn_done, power_set = sem("var_done"), sem("rstd_done"), sem("xn_done"), sem("power_set")
        tx_done, xh_done, xl_done = sem("tx_done"), sem("xh_done"), sem("xl_done")
        gwh_done, gwl_done = sem("gwh_done"), sem("gwl_done")
        rl_done, lg_done, rt_done, L_done = sem("rl_done"), sem("lg_done"), sem("rt_done"), sem("L_done")
        shifted, exp_done, cc_done, ct_t, ct_done = sem("shifted"), sem("exp_done"), sem("cc_done"), sem("ct_t"), sem("ct_done")
        wh_done, w_done = sem("wh_done"), sem("w_done")
        fc_done, s_done, t_done, hf_done, hh_done, hl_done = (sem(k) for k in ("fc_done", "s_done", "t_done", "hf_done", "hh_done", "hl_done"))
        ymm_done, added = sem("ymm_done"), sem("added")
        CH = FT // 2
        TURNS = CH // 2
        LAST = 2 * G * CH
        block = mem.enter_context(nc.Block())

        @block.sync
        def _(sp):
            def piece(f, slot, used):
                if used is not None:
                    sp.wait_ge(w_done, used)
                sp.dma_start(raw[:, slot, :], wc_dram[f, :, :]).then_inc(raw_in[slot], 16)
                sp.dma_start(sraw[:, slot, :], sel_dram[f, :, :]).then_inc(sraw_in[slot], 16)

            sp.dma_start(graw[:, :, :], gate_dram).then_inc(const_in, 16)
            sp.dma_start(key[:, :], key_dram).then_inc(const_in, 16)
            for f in range(4):
                piece(f, f % 2, f - 1 if f >= 2 else None)
            with sp.Fori(0, TURNS - 1) as it:
                for k in range(4):
                    piece(it * 4 + (4 + k), k % 2, it * 4 + (3 + k))
            piece(FT - 1, 0, FT - 2)
            for g in range(G):
                sp.wait_ge(added, (CH * G + g) * 4 + 5)
                sp.dma_start(out_dram[:, 4 * g:4 * g + 4, :], X[:, 4 * g:4 * g + 4, :]).then_inc(out_done, 16)
            sp.wait_ge(out_done, 16 * G)

        @block.gpsimd
        def _(pool):
            def split(f, slot, wslot, raws, used):
                pool.wait_ge(raw_in[slot], raws)
                pool.wait_ge(sraw_in[slot], raws)
                if used is not None:
                    pool.wait_ge(ymm_done, used * 4)
                nc.gpsimd.tensor_tensor(wh[:, wslot, :], raw[:, slot, :], zero[:, :].to_broadcast([P, PW]), ALU.add)
                nc.gpsimd.tensor_tensor(sel[:, wslot, :], sraw[:, slot, :], zero[0:32, :].to_broadcast([32, P]), ALU.add)\
                    .then_inc(wh_done, 1)
                pool.wait_ge(wh_done, f + 1)
                nc.gpsimd.tensor_tensor(wl[:, wslot, :], raw[:, slot, :], as_f32(wh[:, wslot, :]), ALU.subtract)\
                    .then_inc(w_done, 1)

            nc.gpsimd.memset(power[:, :], -0.5).then_inc(power_set, 1)
            nc.gpsimd.memset(zero[:, :], 0.0).then_inc(power_set, 1)
            pool.wait_ge(power_set, 2)
            for f in range(2):
                split(f, f % 2, f, 16, None)
            with pool.Fori(0, G) as g:
                pool.wait_ge(var_done, g + 1)
                nc.gpsimd.tensor_tensor(rstd[:, :], var[:, :], power[:, :].to_broadcast([P, 4]), ALU.pow).then_inc(rstd_done, 1)
            for f in range(2, 4):
                split(f, f % 2, f, 32, None)
            with pool.Fori(0, TURNS - 1) as it:
                for k in range(4):
                    split(it * 4 + (4 + k), k % 2, k, it * 32 + (3 + k // 2) * 16, it * 8 + (6 + 4 * (k // 2)))
            split(FT - 1, 0, 0, (FT // 2 + 1) * 16, (CH - 2) * G + 6)

        @block.vector
        def _(dve):
            own = Chain(dve, own_sem)
            dve.sem_inc(xl_done, 4)
            dve.sem_inc(t_done, 1)
            dve.sem_inc(added, 1)
            dve.sem_inc(ymm_done, 8)
            dve.wait_ge(const_in, 32)
            dve.wait_ge(gwh_done, 1)
            nc.vector.tensor_tensor(gwl[:, :, :], graw[:, :, :], as_f32(gwh[:, :, :]), ALU.subtract).then_inc(gwl_done, 1)
            OWN = 2
            with dve.Fori(0, G) as g:
                loop = Chain(dve, own_sem, OWN, g)
                for k in range(4):
                    last = nc.vector.bn_stats(out=st[:, k, :], in_=X[:, g * 4 + k, :])
                loop.step(last)
                nc.vector.tensor_copy(spare[:, :], st[:, 0, 0:1])
                for k in range(4):
                    last = nc.vector.bn_aggr(out=mv[:, k, :], in_=st[:, k, :])
                loop.step(last)
                assert loop.n == OWN
                nc.vector.tensor_scalar(var[:, :], mv[:, :, 1], EPS, None, ALU.add).then_inc(var_done, 1)
                dve.wait_ge(rstd_done, g + 1)
                for k in range(4):
                    nc.vector.tensor_scalar(xn[:, k, :], X[:, g * 4 + k, :], mv[:, k, 0:1], rstd[:, k:k + 1],
                                            ALU.subtract, ALU.mult).then_inc(xn_done, 1)
                for k in range(4):
                    dve.wait_ge(xh_done, g * 4 + (k + 1))
                    at = bass.ts(g * 4 + k, P)
                    nc.vector.tensor_tensor(xl[:, :, at], tp[:, k, :].rearrange("p (m s) -> p m s", s=P), as_f32(xh[:, :, at]),
                                            ALU.subtract).then_inc(xl_done, 1)
                dve.wait_ge(rt_done, g + 1)
                nc.vector.tensor_copy(L[:, bass.ts(g, 4), :], rt[:, :, 0:16]).then_inc(L_done, 1)
            own.n = OWN * G

            def wide(a):
                return a[:, :].rearrange("p (t o) -> p t o", o=1).to_broadcast([P, NT, E])

            dve.wait_ge(L_done, G)
            own.step(nc.vector.tensor_reduce(out=top[:, :], in_=L[:, :, 0:E], op=ALU.max, axis=AX.X))
            nc.vector.tensor_tensor(prob[:, :, :], L[:, :, 0:E], wide(top), ALU.subtract).then_inc(shifted, 1)
            dve.wait_ge(exp_done, 1)
            own.step(nc.vector.tensor_reduce(out=den[:, :], in_=prob[:, :, :], op=ALU.add, axis=AX.X))
            own.step(nc.vector.reciprocal(den[:, :], den[:, :]))
            own.step(nc.vector.tensor_tensor(prob[:, :, :], prob[:, :, :], wide(den), ALU.mult))
            keys = key[:, :].rearrange("p (o e) -> p o e", o=1).to_broadcast([P, NT, E])
            own.step(nc.vector.tensor_copy(work[:, :, :], prob[:, :, :]))
            for k in range(2):
                own.step(nc.vector.tensor_reduce(out=top[:, :], in_=work[:, :, :], op=ALU.max, axis=AX.X))
                own.step(nc.vector.tensor_tensor(hit[:, :, :], work[:, :, :], wide(top), ALU.is_equal))
                own.step(nc.vector.tensor_tensor(hit[:, :, :], hit[:, :, :], keys, ALU.mult))
                own.step(nc.vector.tensor_reduce(out=top[:, :], in_=hit[:, :, :], op=ALU.max, axis=AX.X))
                mark = chosen if k == 0 else hit
                own.step(nc.vector.tensor_tensor(mark[:, :, :], hit[:, :, :], wide(top), ALU.is_equal))
                if k == 0:
                    own.step(nc.vector.scalar_tensor_tensor(out=work[:, :, :], in0=chosen[:, :, :], scalar=-2.0, in1=prob[:, :, :],
                                                            op0=ALU.mult, op1=ALU.add))
            own.step(nc.vector.tensor_tensor(chosen[:, :, :], chosen[:, :, :], hit[:, :, :], ALU.add))
            own.step(nc.vector.tensor_tensor(prob[:, :, :], prob[:, :, :], chosen[:, :, :], ALU.mult))
            own.step(nc.vector.tensor_scalar(shared[:, :], shared[:, :], 1.0, None, ALU.add))
            own.step(nc.vector.reciprocal(shared[:, :], shared[:, :]))
            own.step(nc.vector.memset(cc[:, :, :], 0.0))
            hi = cc[:, :, 0:GATES].bitcast(FP32R)
            nc.vector.tensor_copy(hi[:, :, 0:E], prob[:, :, :])
            own.step(nc.vector.tensor_copy(hi[:, :, E:GATES].rearrange("p t o -> p (t o)"), shared[:, :]))
            nc.vector.tensor_tensor(cc[:, :, 16:16 + E], prob[:, :, :], cc[:, :, 0:E], ALU.subtract)
            nc.vector.tensor_tensor(cc[:, :, 16 + E:16 + GATES].rearrange("p t o -> p (t o)"), shared[:, :],
                                    cc[:, :, E:GATES].rearrange("p t o -> p (t o)"), ALU.subtract).then_inc(cc_done, 1)
            dve.wait_ge(ct_t, 1)
            nc.vector.tensor_copy(cT[:, :], tp[0:32, :, :].rearrange("p k c -> p (k c)")).then_inc(ct_done, 1)

            def hidden(n, par):
                dve.wait_ge(s_done, n + 1)
                nc.vector.tensor_tensor(t[:, :], s[:, par, :], fc[:, par, 1, :], ALU.mult).then_inc(t_done, 1)
                dve.wait_ge(t_done, n + 2)
                nc.vector.tensor_tensor(hf[:, par, :], t[:, :], gate[:, :], ALU.mult).then_inc(hf_done, 1)

            def low(n, par, slot):
                dve.wait_ge(hh_done, n + 1)
                nc.vector.tensor_tensor(hl[:, slot, :], hf[:, par, :], as_f32(hh[:, slot, :]), ALU.subtract).then_inc(hl_done, 1)

            def add(q, g, k):
                dve.wait_ge(ymm_done, q * 4 + (k + 9))
                tile = X[:, 4 * g + k, :]
                nc.vector.tensor_tensor(tile, tile, yp[:, k % 3, :], ALU.add).then_inc(added, 1)

            hidden(0, 0)
            low(0, 0, 0)
            with dve.Fori(0, TURNS) as it:
                for qq in range(2 * G):
                    q = it * (2 * G) + qq
                    hidden(q * 2 + 1, 1)
                    low(q * 2 + 1, 1, (2 * qq + 1) % 4)
                    hidden(q * 2 + 2, 0)
                    add(q, qq % G, 0)
                    low(q * 2 + 2, 0, (2 * qq + 2) % 4)
                    for k in range(1, 4):
                        add(q, qq % G, k)
            for g in range(G):
                n = LAST + g
                if g:
                    hidden(n, n % 2)
                    low(n, n % 2, n % 4)
                    for k in range(4):
                        add(CH * G + g - 1, g - 1, k)
            for k in range(4):
                add(CH * G + G - 1, G - 1, k)

        @block.scalar
        def _(act):
            act.wait_ge(const_in, 32)
            nc.scalar.copy(gwh[:, :, :], graw[:, :, :]).then_inc(gwh_done, 1)
            with act.Fori(0, G) as g:
                for k in range(4):
                    act.wait_ge(tx_done, g * 4 + (k + 1))
                    nc.scalar.copy(xh[:, :, bass.ts(g * 4 + k, P)], tp[:, k, :].rearrange("p (m s) -> p m s", s=P)).then_inc(xh_done, 1)
                act.wait_ge(rl_done, g + 1)
                nc.scalar.copy(lg[:, :], rl[:, :]).then_inc(lg_done, 1)
            act.wait_ge(shifted, 1)
            act.wait_ge(L_done, G)
            nc.scalar.activation(prob[:, :, :], prob[:, :, :], ACT.Exp)
            nc.scalar.activation(shared[:, :], L[:, :, E], ACT.Exp, scale=-1.0).then_inc(exp_done, 1)

            def silu(n, par):
                act.wait_ge(fc_done, n + 1)
                if not (isinstance(n, int) and n < 2):
                    act.wait_ge(t_done, n)
                nc.scalar.activation(s[:, par, :], fc[:, par, 0, :], ACT.Silu).then_inc(s_done, 1)

            def high(n, par, slot, used):
                act.wait_ge(hf_done, n + 1)
                act.wait_ge(ymm_done, used * 4)
                nc.scalar.copy(hh[:, slot, :], hf[:, par, :]).then_inc(hh_done, 1)

            silu(0, 0)
            high(0, 0, 0, 1)
            with act.Fori(0, TURNS) as it:
                for qq in range(2 * G):
                    q = it * (2 * G) + qq
                    silu(q * 2 + 1, 1)
                    high(q * 2 + 1, 1, (2 * qq + 1) % 4, q + 1)
                    silu(q * 2 + 2, 0)
                    high(q * 2 + 2, 0, (2 * qq + 2) % 4, q + 2)
            for n in range(LAST + 1, LAST + G):
                silu(n, n % 2)
                high(n, n % 2, n % 4, n // 2 + 1)

        @block.tensor
        def _(pe):
            pe.wait_ge(gwl_done, 1)
            with pe.Fori(0, G) as g:
                for k in range(4):
                    pe.wait_ge(xn_done, g * 4 + (k + 1))
                    pe.wait_ge(xl_done, g * 4 + (k + 1))
                    for m in range(KT):
                        last = nc.tensor.transpose(tp[:, k, m * P:(m + 1) * P], xn[:, k, m * P:(m + 1) * P], ident[:, :])
                    last.then_inc(tx_done, 1)
                pe.wait_ge(xl_done, g * 4 + 8)
                at = bass.ts(g, C)
                for m in range(KT):
                    last = matmul3(nc, rl[:, :], (gwh[:, m, :], gwl[:, m, :]), (xh[:, m, at], xl[:, m, at]), m == 0, m == KT - 1)
                last.then_inc(rl_done, 1)
                pe.wait_ge(lg_done, g + 1)
                for k in range(4):
                    last = nc.tensor.transpose(rt[:, k, :], lg[:, k * P:(k + 1) * P], ident[:, :])
                last.then_inc(rt_done, 1)
            pe.wait_ge(cc_done, 1)
            for k in range(NT):
                last = nc.tensor.transpose(tp[:, k // 4, (k % 4) * P:(k % 4 + 1) * P], cc[:, k, :], ident[:, :])
            last.then_inc(ct_t, 1)
            pe.wait_ge(ct_done, 1)

            def products(n, par, g, slot, pieces):
                if pieces is not None:
                    pe.wait_ge(w_done, pieces)
                if not (isinstance(n, int) and n < 2):
                    pe.wait_ge(t_done, n)
                at = slice(g * C, (g + 1) * C)
                for half in range(2):
                    for m in range(KT):
                        o = half * C + m * P
                        matmul3(nc, fc[:, par, half, :], (wh[:, slot, o:o + P], wl[:, slot, o:o + P]),
                                (xh[:, m, at], xl[:, m, at]), m == 0, m == KT - 1)
                if not (isinstance(n, int) and n == 0):
                    pe.wait_ge(hf_done, n)
                nc.tensor.matmul(gate[:, :], sel[:, slot, :], cT[:, at], start=True, stop=True).then_inc(fc_done, 1)

            def project(q, units, slots, wslots):
                pe.wait_ge(hl_done, units)
                for k in range(4):
                    if k == 0:
                        pe.wait_ge(added, q * 4 + 1)
                    if k == 3:
                        pe.wait_ge(added, q * 4 + 2)
                    for i, (hs, ws) in enumerate(zip(slots, wslots)):
                        a = slice(k * P, (k + 1) * P)
                        last = matmul3(nc, yp[:, k % 3, :], (hh[:, hs, a], hl[:, hs, a]),
                                       (wh[:, ws, 2 * C:PW], wl[:, ws, 2 * C:PW]), i == 0, i == len(slots) - 1)
                    last.then_inc(ymm_done, 1)

            products(0, 0, 0, 0, 1)
            with pe.Fori(0, TURNS) as it:
                for qq in range(2 * G):
                    q = it * (2 * G) + qq
                    c = qq // G
                    products(q * 2 + 1, 1, qq % G, 2 * c + 1, it * 4 + (2 * c + 2) if qq % G == 0 else None)
                    nxt = (qq + 1) // G
                    products(q * 2 + 2, 0, (qq + 1) % G, (2 * nxt) % 4, it * 4 + (2 * nxt + 1) if (qq + 1) % G == 0 else None)
                    project(q, q * 2 + 2, ((2 * qq) % 4, (2 * qq + 1) % 4), (2 * c, 2 * c + 1))
            for g in range(1, G):
                products(LAST + g, g % 2, g, 0, None)
                project(CH * G + g - 1, LAST + g, ((LAST + g - 1) % 4,), (0,))
            project(CH * G + G - 1, LAST + G, ((LAST + G - 1) % 4,), (0,))


PAIRED = [2 * i + c for c in range(2) for i in range(ROT // 2)] + list(range(ROT, RD))


def retention_tables():
    j = np.arange(P)[:, None]
    near = np.concatenate([np.arange(S)[None, :] - j, np.arange(P)[None, :] - j], 1)
    gamma = 1.0 - 2.0 ** (-5.0 - np.arange(RH, dtype=np.float64))
    decay = np.where(near[:, None, :] >= 0, gamma[None, :, None] ** np.maximum(near, 0)[:, None, :], 0.0)
    t = np.arange(S, dtype=np.float32)
    inv = (np.float32(1.0) / np.float32(10000.0) ** (np.arange(0, ROT, 2, dtype=np.float32) / np.float32(ROT))).astype(np.float32)
    angle = np.repeat((t[:, None] * inv[None, :]).astype(np.float32), 2, -1).astype(np.float64)
    base = (np.arange(0, ROT, 2) + 0.4 * ROT) / (1.4 * ROT)
    scale = base[None, :] ** ((t.astype(np.float64) - S // 2) / 512.0)[:, None]
    scale = np.concatenate([scale, scale], -1)
    sign = np.where(np.arange(ROT) % 2 == 0, -1.0, 1.0)
    rot = np.stack([np.stack([np.cos(angle) * s, np.sin(angle) * s * sign]) for s in (scale, 1.0 / scale)])
    rot = rot[..., PAIRED[:ROT]].reshape(2, 2, TB, P, ROT).transpose(3, 2, 0, 1, 4)
    return decay.astype(np.float32), np.ascontiguousarray(rot.astype(np.float32))


def tiles(w):
    return w.reshape(-1, P, w.shape[1]).transpose(1, 0, 2)


def layout_retention(i):
    qkv = i["L0_attn_wqkv"].T.reshape(C, RH, 3, RD)
    q, k, v = qkv[:, :, 0][..., PAIRED], qkv[:, :, 1][..., PAIRED], qkv[:, :, 2]
    w = np.concatenate([a.reshape(C, C) for a in (q, k, v)] + [i["L0_attn_wg"].T], 1).reshape(KT, P, 4 * C)
    wo = tiles(i["L0_attn_wo"].T).reshape(1, P, KT * C)
    decay, rot = retention_tables()
    gn = np.stack([np.repeat(i[k], RD).reshape(KT, P).T for k in ("L0_attn_gn_weight", "L0_attn_gn_bias")], 1)
    blk = np.kron(np.eye(P // RD), np.full((RD, RD), 1.0 / RD)).astype(np.float32)
    return {"a_w": np.concatenate([w, wo], 0), "a_decay": decay, "a_rot": rot, "a_gn": gn, "a_blk": blk}


def layout_feed_forward(i):
    f1 = np.concatenate([i["L0_ffn_expert_fc1"].reshape(E * FE, C), i["L0_ffn_shared_fc1"]], 0)
    f2 = np.concatenate([i["L0_ffn_expert_fc2"].reshape(E * FE, C), i["L0_ffn_shared_fc2"]], 0)
    pr = np.concatenate([i["L0_ffn_expert_proj"].transpose(0, 2, 1).reshape(E * FE, C), i["L0_ffn_shared_proj"].T], 0)
    ups = [w.reshape(FT, P, KT, P).transpose(0, 3, 2, 1).reshape(FT, P, C) for w in (f1, f2)]
    w = np.concatenate(ups + [pr.reshape(FT, P, C)], 2)
    owner = np.minimum(np.arange(FT * P) // FE, E).reshape(FT, 1, P)
    sel = (owner == np.arange(16)[None, :, None]).astype(np.float32)
    sel = np.concatenate([sel, sel], 1)
    gates = np.zeros((C, P), np.float32)
    gates[:, :E] = i["L0_ffn_gate_w"].T
    gates[:, E] = i["L0_ffn_shared_gate_w"][0]
    key = np.tile(np.arange(E, 0, -1, dtype=np.float32), (P, 1))
    return {"c_w": w, "c_sel": sel, "c_gate": tiles(gates), "c_key": key}


def layout_attention(i):
    def apart(w):
        return w.reshape(-1, XH, 2, 4, 2).transpose(0, 4, 1, 2, 3).reshape(-1, C)

    kv = np.concatenate([apart(i["L0_xattn_Wkv"][:, :C]), i["L0_xattn_Wkv"][:, C:]], 1)
    w = np.stack([tiles(a).reshape(P, 2048) for a in (apart(i["L0_xattn_Wq"]), kv, i["L0_xattn_Wout"])])
    ctx = i["ctx_1024"].reshape(B, S, CKT, P).transpose(0, 3, 2, 1)
    pos = i["fside_BxSx2_0"].reshape(NT, P, 2).transpose(1, 0, 2)
    freq = np.tile(np.float32(10000.0) ** (-np.arange(4, dtype=np.float32) / np.float32(4)), (P, 2, 1)).astype(np.float32)
    bout = np.broadcast_to(i["L0_xattn_bout"], (P, C))
    return {"b_w": w, "b_ctx": ctx, "b_pos": pos, "b_freq": freq, "b_bout": bout}


def decoder_layer(nc, ins, out_dram):
    with ExitStack() as mem:
        X = mem.enter_context(nc.sbuf_tensor("residual", [P, NT, C], FP32))
        ident = mem.enter_context(nc.sbuf_tensor("identity", [P, P], FP32))
        retention(nc, X, ins["x"], ins["a_w"], ins["a_decay"], ins["a_rot"], ins["a_gn"], ins["a_blk"], ident, ins["ident"])
        cross_attention(nc, X, ins["b_w"], ins["b_ctx"], ins["b_pos"], ins["b_freq"], ins["b_bout"], ident)
        feed_forward(nc, X, ins["c_w"], ins["c_sel"], ins["c_gate"], ins["c_key"], ident, out_dram)


def kernel(**inputs):
    import concourse.bacc as bacc
    from concourse.bass_utils import run_bass_kernel_spmd

    i = {k: np.asarray(v) for k, v in inputs.items()}
    arrays = {"x": tiles(i["x"].reshape(B * S, C)), "ident": np.eye(P, dtype=np.float32)}
    arrays |= layout_retention(i) | layout_attention(i) | layout_feed_forward(i)
    nc = bacc.Bacc("TRN2", target_bir_lowering=False, num_devices=1)
    feeds, ins = {}, {}
    for name, a in arrays.items():
        feeds[f"in_{name}"] = np.ascontiguousarray(a)
        ins[name] = nc.dram_tensor(f"in_{name}", a.shape, mybir.dt.from_np(a.dtype), kind="ExternalInput").ap()
    out = nc.dram_tensor("out_0", (P, NT, C), FP32, kind="ExternalOutput").ap()
    decoder_layer(nc, ins, out)
    r = run_bass_kernel_spmd(nc, [feeds], core_ids=[0])
    return r.results[0]["out_0"].transpose(1, 0, 2).reshape(B, S, C)
```

```python
from contextlib import ExitStack

import concourse.bass as bass
import numpy as np
from concourse import mybir

FP32 = mybir.dt.float32
FP32R = mybir.dt.float32r
FP16 = mybir.dt.float16
BF16 = mybir.dt.bfloat16
ALU = mybir.AluOpType
ACT = mybir.ActivationFunctionType
AX = mybir.AxisListType

P = 128
B, S, C = 8, 256, 512
NT = B * S // P
TB = S // P
KT = C // P
EPS = 1e-5

RH, RD, ROT = 8, 64, 32
XH, XD, CTXW = 32, 16, 256
CKT = CTXW // P
E, FE, FS = 8, 352, 1408
GATES = E + 1
FT = (E * FE + FS) // P


def as_f32(ap):
    return ap.bitcast(FP32)


def matmul3(nc, out, left, right, start, stop):
    (lh, ll), (rh, rl) = left, right
    nc.tensor.matmul(out, ll, rh, start=start, stop=False)
    nc.tensor.matmul(out, lh, rl, start=False, stop=False)
    return nc.tensor.matmul(out, lh, rh, start=False, stop=stop)


class Chain:

    def __init__(self, engine, sem, per=0, turn=0, base=0):
        self.engine, self.sem, self.per, self.turn, self.base, self.n = engine, sem, per, turn, base, 0

    def step(self, instruction):
        instruction.then_inc(self.sem, 1)
        self.n += 1
        self.engine.wait_ge(self.sem, self.turn * self.per + (self.base + self.n))


def retention(nc, X, x_dram, wa_dram, decay_dram, rot_dram, gn_dram, blk_dram, ident, ident_dram):
    with ExitStack() as mem:
        def sb(name, shape, dt=FP32):
            return mem.enter_context(nc.sbuf_tensor("a_" + name, shape, dt))

        def sem(name):
            return nc.alloc_semaphore("a_" + name)

        with nc.sbuf_tensor("a_raw", [P, 2, 2048], FP32) as raw:
            pass
        qh, ql = sb("qh", [P, KT, S], FP32R), sb("ql", [P, KT, S], FP32R)
        kh, kl = sb("kh", [P, KT, S], FP32R), sb("kl", [P, KT, S], FP32R)
        wh, wl = sb("wh", [P, 5, 2048], FP32R), sb("wl", [P, 5, 2048], FP32R)
        decay = sb("decay", [P, RH, 384])
        rot = sb("rot", [P, TB, 2, 2, ROT])
        gn = sb("gn", [P, 2, KT])
        blk = sb("blk", [P, P])
        xn = sb("xn", [P, TB, C])
        st, mv = sb("st", [P, TB, 6]), sb("mv", [P, TB, 2])
        var, rstd, spare = sb("var", [P, TB]), sb("rstd", [P, TB]), sb("spare", [P, 1])
        two, power = sb("two", [P, 1]), sb("power", [P, 1])
        xh, xl = sb("xh", [P, KT, S], FP32R), sb("xl", [P, KT, S], FP32R)
        qk = sb("qk", [P, 2, TB, C])
        t1, t2 = (xn[:, t, 0:RH * ROT].rearrange("p (h d) -> p h d", h=RH) for t in range(TB))
        vraw = sb("vraw", [P, TB, C])
        vh, vl = sb("vh", [P, TB, RH, P], FP32R), sb("vl", [P, TB, RH, P], FP32R)
        graw = sb("graw", [P, KT, S])
        u = sb("u", [P, KT, S])
        with nc.sbuf_tensor("a_gcn", [P, 2, KT, S], FP32) as gcn:
            gc, n = gcn[:, 0, :, :], gcn[:, 1, :, :]
        zh, zl = sb("zh", [P, KT, S], FP32R), sb("zl", [P, KT, S], FP32R)
        sd = sb("sd", [P, 2, 384])
        sh, sl = sb("sh", [P, 2, 384], FP32R), sb("sl", [P, 2, 384], FP32R)
        gst, gmv = sb("gst", [P, KT, 6]), sb("gmv", [P, KT, 2])
        gsq, gm = sb("gsq", [P, KT, 1]), sb("gm", [P, KT, 2])
        gvar, ga, gb = sb("gvar", [P, KT]), sb("ga", [P, KT]), sb("gb", [P, KT])
        d, mish = u, n
        y, z = gc, u

        def pb(name, shape):
            return mem.enter_context(nc.psum_tensor("a_" + name, shape, FP32))

        tp = pb("tp", [P, KT, S])
        gemm = pb("gemm", [P, 2, C])
        sc = pb("sc", [P, 2, 512])
        rt = pb("rt", [P, KT, S])

        x0_in, x_in = sem("x0_in"), sem("x_in")
        const_in = sem("const_in")
        raw_in = [sem("raw_in0"), sem("raw_in1")]
        wh_done, wl_done = sem("wh_done"), sem("wl_done")
        pads = sem("pads_zeroed")
        dve_own = sem("dve_own")
        var_done, rstd_done, gvar_done, gpow_done = sem("var_done"), sem("rstd_done"), sem("gvar_done"), sem("gpow_done")
        xn_done, tx_done, xh_done = sem("xn_done"), sem("tx_done"), sem("xh_done")
        xl_done = sem("xl_done")
        gemm_done, gemm_act = sem("gemm_done"), sem("gemm_act")
        rot_done, rot_added = sem("rot_done"), sem("rot_added")
        tq_done, tk_done, qh_done, kh_done = sem("tq_done"), sem("tk_done"), sem("qh_done"), sem("kh_done")
        ql_done, kl_done = sem("ql_done"), sem("kl_done")
        vh_done, vl_done = sem("vh_done"), sem("vl_done")
        sc_done, sd_done, sh_done, sl_done = sem("sc_done"), sem("sd_done"), sem("sh_done"), sem("sl_done")
        ret_done, tm_done = sem("ret_done"), sem("tm_done")
        gc_done, u_done, n_done, d_done, mish_done = (sem(k) for k in ("gc_done", "u_done", "n_done", "d_done", "mish_done"))
        gst_done, gmm_done, gmm_read, coef_done = sem("gst_done"), sem("gmm_done"), sem("gmm_read"), sem("coef_done")
        y_done, z_done, zh_done, zl_done = sem("y_done"), sem("z_done"), sem("zh_done"), sem("zl_done")
        wo_done, added = sem("wo_done"), sem("added")
        NPIECE = 5
        block = mem.enter_context(nc.Block())

        @block.sync
        def _(sp):
            sp.dma_start(X[:, 0:TB, :], x_dram[:, 0:TB, :]).then_inc(x0_in, 16)
            for k in range(NPIECE):
                if k >= 2:
                    sp.wait_ge(wl_done, k - 1)
                sp.dma_start(raw[:, k % 2, :], wa_dram[k, :, :]).then_inc(raw_in[k % 2], 16)
                if k == 1:
                    sp.dma_start(ident[:, :], ident_dram).then_inc(const_in, 16)
                    sp.dma_start(rot[:, :, :, :, :], rot_dram).then_inc(const_in, 16)
                    sp.dma_start(gn[:, :, :], gn_dram).then_inc(const_in, 16)
                    sp.dma_start(blk[:, :], blk_dram).then_inc(const_in, 16)
                    sp.dma_start(decay[:, :, :], decay_dram).then_inc(const_in, 16)
            sp.dma_start(X[:, TB:NT, :], x_dram[:, TB:NT, :]).then_inc(x_in, 16)

        @block.tensor
        def _(pe):
            def transpose_x(b, first):
                pe.wait_ge(xn_done, b + 1)
                if not first:
                    pe.wait_ge(ql_done, b)
                for t in range(TB):
                    for k in range(KT):
                        last = nc.tensor.transpose(tp[:, k, t * P:(t + 1) * P], xn[:, t, k * P:(k + 1) * P], ident[:, :])
                last.then_inc(tx_done, 1)

            def gemm_chunk(b, c, first, ks=range(KT)):
                if 0 in ks and (not first or c >= 2):
                    if first:
                        pe.wait_ge(gemm_act, c - 1)
                        pe.wait_ge(rot_done, min(c - 1, 4))
                    else:
                        pe.wait_ge(gemm_act, b * 8 + (c - 1 if c >= 2 else 0))
                        pe.wait_ge(rot_done, b * 4 + (min(c - 1, 4) if c >= 2 else 0))
                        if c < 2:
                            pe.wait_ge(added, b * 2 - 1)
                bank = gemm[:, c % 2, :]
                t, o = c % 2, (c // 2) * C
                for k in ks:
                    if first and c == 0:
                        pe.wait_ge(wl_done, k + 1)
                    last = matmul3(nc, bank, (xh[:, k, t * P:(t + 1) * P], xl[:, k, t * P:(t + 1) * P]),
                                   (wh[:, k, o:o + C], wl[:, k, o:o + C]), k == 0, k == KT - 1)
                if KT - 1 in ks:
                    last.then_inc(gemm_done, 1)

            def scores(b, h):
                pe.wait_ge(sd_done, b * 8 + h + 1)
                r, m = (h % 2) * RD, h // 2
                kk, qq = (kh[r:r + RD, m, :], kl[r:r + RD, m, :]), (qh[r:r + RD, m, :], ql[r:r + RD, m, :])
                matmul3(nc, sc[:, h % 2, 0:S], [a[:, 0:P] for a in kk], qq, True, True)
                matmul3(nc, sc[:, h % 2, S:384], [a[:, P:S] for a in kk], [a[:, P:S] for a in qq], True, True)\
                    .then_inc(sc_done, 1)

            def ret(b, h):
                pe.wait_ge(sh_done, b * 8 + h + 1)
                pe.wait_ge(sl_done, b * 8 + h + 3)
                m = h // 2
                first = h % 2 == 0
                matmul3(nc, rt[:, m, :], (vh[:, 0, h, :], vl[:, 0, h, :]), (sh[:, h % 2, 0:S], sl[:, h % 2, 0:S]), first, False)
                matmul3(nc, rt[:, m, P:S], (vh[:, 1, h, :], vl[:, 1, h, :]), (sh[:, h % 2, S:384], sl[:, h % 2, S:384]),
                        False, not first).then_inc(ret_done, 1)

            def transpose_qk(b):
                pe.wait_ge(rot_added, b * 4 + 4)
                pe.wait_ge(gemm_act, b * 8 + 8)
                pe.wait_ge(xl_done, b + 1)
                pe.wait_ge(gmm_read, b + 1)
                for t in range(TB):
                    for k in range(KT):
                        last = nc.tensor.transpose(tp[:, k, t * P:(t + 1) * P], qk[:, 0, t, k * P:(k + 1) * P], ident[:, :])
                last.then_inc(tq_done, 1)
                pe.wait_ge(y_done, b + 1)
                for t in range(TB):
                    for k in range(KT):
                        last = nc.tensor.transpose(rt[:, k, t * P:(t + 1) * P], qk[:, 1, t, k * P:(k + 1) * P], ident[:, :])
                last.then_inc(tk_done, 1)

            def body(b, nxt):
                if nxt:
                    transpose_x(b + 1, False)
                pe.wait_ge(ql_done, b + 1)
                pe.wait_ge(kl_done, b + 1)
                scores(b, 0)
                for h in range(RH):
                    if h + 1 < RH:
                        scores(b, h + 1)
                    if nxt:
                        if h == 0:
                            pe.wait_ge(xl_done, b + 2)
                        gemm_chunk(b + 1, h // 2, False, (2 * (h % 2), 2 * (h % 2) + 1))
                    if h == 1:
                        pe.wait_ge(vh_done, b + 1)
                        pe.wait_ge(vl_done, b + 1)
                    if h >= 1:
                        ret(b, h - 1)
                if nxt:
                    gemm_chunk(b + 1, 4, False, (0, 1))
                ret(b, RH - 1)
                if nxt:
                    gemm_chunk(b + 1, 4, False, (2, 3))
                    gemm_chunk(b + 1, 5, False)
                pe.wait_ge(gst_done, b + 1)
                nc.tensor.matmul(tp[:, 0, 0:2 * KT], blk[:, :], gm[:, :, :], start=True, stop=True).then_inc(gmm_done, 1)
                if nxt:
                    gemm_chunk(b + 1, 6, False)
                pe.wait_ge(mish_done, b + 1)
                pe.wait_ge(sd_done, b * 8 + 10)
                for t in range(TB):
                    for k in range(KT):
                        last = nc.tensor.transpose(sc[:, k // 2, k % 2 * S + t * P:k % 2 * S + (t + 1) * P],
                                                   mish[:, 2 * t + k // 2, k % 2 * P:(k % 2 + 1) * P], ident[:, :])
                last.then_inc(tm_done, 1)
                if nxt:
                    gemm_chunk(b + 1, 7, False)
                    transpose_qk(b + 1)
                pe.wait_ge(zh_done, b + 1)
                pe.wait_ge(zl_done, b + 2)
                for t in range(TB):
                    if nxt:
                        pe.wait_ge(gemm_act, b * 8 + 15 + t)
                    else:
                        pe.wait_ge(added, b * 2 + 1)
                    for k in range(KT):
                        last = matmul3(nc, gemm[:, t, :], (zh[:, k, t * P:(t + 1) * P], zl[:, k, t * P:(t + 1) * P]),
                                       (wh[:, 4, k * C:(k + 1) * C], wl[:, 4, k * C:(k + 1) * C]), k == 0, k == KT - 1)
                    last.then_inc(wo_done, 1)

            pe.wait_ge(const_in, 80)
            transpose_x(0, True)
            pe.wait_ge(xl_done, 1)
            for c in range(8):
                gemm_chunk(0, c, True)
            pe.wait_ge(wl_done, NPIECE)
            transpose_qk(0)
            with pe.Fori(0, B - 2) as b:
                body(b, True)
            body(B - 2, True)
            body(B - 1, False)

        @block.vector
        def _(dve):
            def layernorm(own, b):
                for t in range(TB):
                    tile = X[:, b * TB + t, :]
                    own.step(nc.vector.bn_stats(out=st[:, t, :], in_=tile))
                nc.vector.tensor_copy(spare[:, :], st[:, 0, 0:1])
                for t in range(TB):
                    last = nc.vector.bn_aggr(out=mv[:, t, :], in_=st[:, t, :])
                own.step(last)
                nc.vector.tensor_scalar(var[:, :], mv[:, :, 1], EPS, None, ALU.add).then_inc(var_done, 1)
                dve.wait_ge(rstd_done, b + 1)
                dve.wait_ge(tx_done, b)
                dve.wait_ge(rot_added, b * 4)
                for t in range(TB):
                    last = nc.vector.tensor_scalar(xn[:, t, :], X[:, b * TB + t, :], mv[:, t, 0:1], rstd[:, t:t + 1],
                                                   ALU.subtract, ALU.mult)
                last.then_inc(xn_done, 1)

            def x_low(b):
                dve.wait_ge(xh_done, b + 1)
                nc.vector.tensor_tensor(xl[:, :, :], tp[:, :, :], as_f32(xh[:, :, :]), ALU.subtract).then_inc(xl_done, 1)

            def rotate(c, gb, first=False):
                dve.wait_ge(gemm_act, gb * 8 + c + 1)
                if not first or c:
                    dve.wait_ge(rot_added, gb * 4 + c)
                t, which = c % 2, c // 2
                src = gemm[:, c % 2, :].rearrange("p (h d) -> p h d", h=RH)
                cos = rot[:, t, which, 0, :].rearrange("p (o d) -> p o d", o=1).to_broadcast([P, RH, ROT])
                sin = rot[:, t, which, 1, :].rearrange("p (o d) -> p o d", o=1).to_broadcast([P, RH, ROT])
                H = ROT // 2
                nc.vector.tensor_tensor(t1[:, :, :], src[:, :, 0:ROT], cos, ALU.mult)
                nc.vector.tensor_tensor(t2[:, :, 0:H], src[:, :, H:ROT], sin[:, :, 0:H], ALU.mult)
                nc.vector.tensor_tensor(t2[:, :, H:ROT], src[:, :, 0:H], sin[:, :, H:ROT], ALU.mult)\
                    .then_inc(rot_done, 1)

            def qk_low(b):
                dve.wait_ge(qh_done, b + 1)
                nc.vector.tensor_tensor(ql[:, :, :], tp[:, :, :], as_f32(qh[:, :, :]), ALU.subtract).then_inc(ql_done, 1)
                dve.wait_ge(kh_done, b + 1)
                nc.vector.tensor_tensor(kl[:, :, :], rt[:, :, :], as_f32(kh[:, :, :]), ALU.subtract).then_inc(kl_done, 1)

            OWN_PROLOGUE, OWN = 3, 12

            def body(b, nxt, norm, base):
                own = Chain(dve, dve_own, 0 if isinstance(b, int) else OWN, b, base)
                dve.wait_ge(gemm_act, b * 8 + 8)
                nc.vector.tensor_scalar(gc[:, :, :], graw[:, :, :], 20.0, None, ALU.min).then_inc(gc_done, 1)
                if nxt:
                    x_low(b + 1)
                for h in range(RH):
                    dve.wait_ge(sc_done, b * 8 + h + 1)
                    dve.wait_ge(sl_done, b * 8 + h + 1)
                    nc.vector.tensor_tensor(sd[:, h % 2, :], sc[:, h % 2, 0:384], decay[:, h, :], ALU.mult).then_inc(sd_done, 1)
                    if nxt and h % 2:
                        rotate(h // 2, b + 1)
                    if h == 0:
                        dve.wait_ge(u_done, b + 1)
                        nc.vector.scalar_tensor_tensor(out=n[:, :, :], in0=u[:, :, :], scalar=2.0, in1=u[:, :, :],
                                                       op0=ALU.add, op1=ALU.mult).then_inc(n_done, 1)
                    if h == 1:
                        dve.wait_ge(d_done, b + 1)
                    for piece in {1: (0, 1)}.get(h, (h,) if h > 1 else ()):
                        half = d[:, piece // 2, piece % 2 * P:(piece % 2 + 1) * P]
                        last = nc.vector.reciprocal(half, half)
                own.step(last)
                dve.wait_ge(ret_done, b * 8 + 10)
                for m in range(KT):
                    last = nc.vector.bn_stats(out=gst[:, m, :], in_=rt[:, m, :])
                own.step(last)
                nc.vector.tensor_copy(spare[:, :], gst[:, 0, 0:1])
                for m in range(KT):
                    last = nc.vector.bn_aggr(out=gmv[:, m, :], in_=gst[:, m, :])
                own.step(last)
                own.step(nc.vector.tensor_tensor(gsq[:, :, :], gmv[:, :, 0:1], gmv[:, :, 0:1], ALU.mult))
                nc.vector.tensor_copy(gm[:, :, 0:1], gmv[:, :, 0:1])
                nc.vector.tensor_tensor(gm[:, :, 1:2], gmv[:, :, 1:2], gsq[:, :, :], ALU.add).then_inc(gst_done, 1)
                own.step(nc.vector.tensor_tensor(n[:, :, :], n[:, :, :], d[:, :, :], ALU.mult))
                nc.vector.tensor_tensor(mish[:, :, :], n[:, :, :], graw[:, :, :], ALU.mult).then_inc(mish_done, 1)
                dve.wait_ge(gmm_done, b + 1)
                nc.vector.tensor_copy(gmv[:, :, :], tp[:, 0, 0:2 * KT].rearrange("p (m s) -> p m s", s=2)).then_inc(gmm_read, 1)
                dve.wait_ge(gmm_read, b + 2)
                own.step(nc.vector.tensor_tensor(gsq[:, :, :], gmv[:, :, 0:1], gmv[:, :, 0:1], ALU.mult))
                own.step(nc.vector.tensor_tensor(gvar[:, :], gmv[:, :, 1], gsq[:, :, 0], ALU.subtract))
                nc.vector.tensor_scalar(gvar[:, :], gvar[:, :], EPS, None, ALU.add).then_inc(gvar_done, 1)
                dve.wait_ge(gpow_done, b + 1)
                own.step(nc.vector.tensor_tensor(ga[:, :], gvar[:, :], gn[:, 0, :], ALU.mult))
                own.step(nc.vector.tensor_tensor(gvar[:, :], gmv[:, :, 0], ga[:, :], ALU.mult))
                nc.vector.tensor_tensor(gb[:, :], gn[:, 1, :], gvar[:, :], ALU.subtract).then_inc(coef_done, 1)
                dve.wait_ge(y_done, b + 2)
                dve.wait_ge(tm_done, b + 1)
                nc.vector.tensor_tensor(z[:, :, :], y[:, :, :], sc[:, :, :].rearrange("p a (b s) -> p (a b) s", s=S), ALU.mult)\
                    .then_inc(z_done, 1)
                if nxt:
                    qk_low(b + 1)
                if norm:
                    layernorm(own, b + 2)
                for t in range(TB):
                    dve.wait_ge(wo_done, b * 2 + t + 1)
                    tile = X[:, b * TB + t, :]
                    nc.vector.tensor_tensor(tile, tile, gemm[:, t, :], ALU.add).then_inc(added, 1)
                return base + own.n

            nc.vector.memset(gst[:, :, :], 0.0).then_inc(sd_done, 2)
            nc.vector.memset(gmv[:, :, :], 0.0).then_inc(gmm_read, 1)
            nc.vector.memset(gm[:, :, :], 0.0).then_inc(added, 1)
            own = Chain(dve, dve_own)
            dve.wait_ge(x0_in, 16)

            def first_norm(b):
                for t in range(TB):
                    tile = X[:, b * TB + t, :]
                    own.step(nc.vector.bn_stats(out=st[:, t, :], in_=tile))
                nc.vector.tensor_copy(spare[:, :], st[:, 0, 0:1])
                for t in range(TB):
                    last = nc.vector.bn_aggr(out=mv[:, t, :], in_=st[:, t, :])
                own.step(last)
                nc.vector.tensor_scalar(var[:, :], mv[:, :, 1], EPS, None, ALU.add).then_inc(var_done, 1)
                dve.wait_ge(rstd_done, b + 1)
                if b:
                    dve.wait_ge(tx_done, b)
                    dve.wait_ge(rot_added, b * 4)
                for t in range(TB):
                    last = nc.vector.tensor_scalar(xn[:, t, :], X[:, b * TB + t, :], mv[:, t, 0:1], rstd[:, t:t + 1],
                                                   ALU.subtract, ALU.mult)
                last.then_inc(xn_done, 1)

            first_norm(0)
            for k in range(NPIECE):
                dve.wait_ge(wh_done, k + 1)
                nc.vector.tensor_tensor(wl[:, k, :], raw[:, k % 2, :], as_f32(wh[:, k, :]), ALU.subtract).then_inc(wl_done, 1)
                if k == 1:
                    x_low(0)
                if k == 3:
                    dve.wait_ge(const_in, 80)
                    for c in range(2):
                        rotate(c, 0, True)
            for c in range(2, 4):
                rotate(c, 0, True)
            dve.wait_ge(x_in, 16)
            first_norm(1)
            assert own.n == OWN_PROLOGUE * 2
            qk_low(0)
            with dve.Fori(0, B - 2) as b:
                steps = body(b, True, True, OWN_PROLOGUE * 2)
            assert steps == OWN_PROLOGUE * 2 + OWN, steps - OWN_PROLOGUE * 2
            steps = body(B - 2, True, False, OWN_PROLOGUE * 2 + (B - 2) * OWN)
            body(B - 1, False, False, steps)

        @block.scalar
        def _(act):
            def chunk_out(c, gb):
                act.wait_ge(gemm_done, gb * 8 + c + 1)
                bank = gemm[:, c % 2, :]
                if c < 4:
                    src = bank.rearrange("p (h d) -> p h d", h=RH)[:, :, ROT:RD]
                    dst = qk[:, c // 2, c % 2, :].rearrange("p (h d) -> p h d", h=RH)[:, :, ROT:RD]
                    nc.scalar.copy(dst, src).then_inc(gemm_act, 1)
                elif c < 6:
                    nc.scalar.copy(vraw[:, c - 4, :], bank).then_inc(gemm_act, 1)
                else:
                    g = 2 * (c - 6)
                    nc.scalar.copy(graw[:, g:g + 2, :].rearrange("p m s -> p (m s)"), bank).then_inc(gemm_act, 1)

            def qk_high(b):
                act.wait_ge(tq_done, b + 1)
                nc.scalar.copy(qh[:, :, :], tp[:, :, :]).then_inc(qh_done, 1)
                act.wait_ge(tk_done, b + 1)
                nc.scalar.copy(kh[:, :, :], rt[:, :, :]).then_inc(kh_done, 1)

            def body(b, nxt):
                if nxt:
                    act.wait_ge(tx_done, b + 2)
                    nc.scalar.copy(xh[:, :, :], tp[:, :, :]).then_inc(xh_done, 1)
                act.wait_ge(gemm_act, b * 8 + 8)
                act.wait_ge(ret_done, b * 8 + 2)
                for e in range(2):
                    dst = vh[:, :, :, e * RD:(e + 1) * RD].rearrange("p t (m e) d -> p t m e d", e=2)[:, :, :, e, :]
                    src = vraw[:, :, :].rearrange("p t (m e d) -> p t m e d", e=2, d=RD)[:, :, :, e, :]
                    last = nc.scalar.copy(dst, src)
                last.then_inc(vh_done, 1)
                act.wait_ge(gc_done, b + 1)
                act.wait_ge(zl_done, b + 1)
                nc.scalar.activation(u[:, :, :], gc[:, :, :], ACT.Exp).then_inc(u_done, 1)
                for h in range(RH):
                    act.wait_ge(sd_done, b * 8 + h + 3)
                    act.wait_ge(ret_done, b * 8 + h + 1)
                    nc.scalar.copy(sh[:, h % 2, :], sd[:, h % 2, :]).then_inc(sh_done, 1)
                    if nxt and h % 2:
                        if h == 1:
                            act.wait_ge(tk_done, b + 1)
                        chunk_out(h // 2, b + 1)
                if nxt:
                    act.wait_ge(vl_done, b + 1)
                    chunk_out(4, b + 1)
                    chunk_out(5, b + 1)
                    act.wait_ge(mish_done, b + 1)
                    chunk_out(6, b + 1)
                act.wait_ge(coef_done, b + 1)
                for m in range(KT):
                    last = nc.scalar.activation(y[:, m, :], rt[:, m, :], ACT.Identity, bias=gb[:, m:m + 1], scale=ga[:, m:m + 1])
                last.then_inc(y_done, 1)
                if nxt:
                    chunk_out(7, b + 1)
                act.wait_ge(z_done, b + 1)
                act.wait_ge(added, b * 2 + 1)
                nc.scalar.copy(zh[:, :, :], z[:, :, :]).then_inc(zh_done, 1)
                if nxt:
                    qk_high(b + 1)

            for k in range(NPIECE):
                act.wait_ge(raw_in[k % 2], 16 * (k // 2 + 1))
                nc.scalar.copy(wh[:, k, :], raw[:, k % 2, :]).then_inc(wh_done, 1)
                if k == 1:
                    act.wait_ge(tx_done, 1)
                    nc.scalar.copy(xh[:, :, :], tp[:, :, :]).then_inc(xh_done, 1)
                if k == 3:
                    chunk_out(0, 0)
                    chunk_out(1, 0)
            for c in range(2, 8):
                chunk_out(c, 0)
            act.wait_ge(wl_done, NPIECE)
            qk_high(0)
            with act.Fori(0, B - 2) as b:
                body(b, True)
            body(B - 2, True)
            body(B - 1, False)

        @block.gpsimd
        def _(pool):
            def flat(a):
                return a[:, :, :].rearrange("p m s -> p (m s)")

            def root(b):
                pool.wait_ge(var_done, b + 1)
                nc.gpsimd.tensor_tensor(rstd[:, :], var[:, :], power[:, :].to_broadcast([P, TB]), ALU.pow).then_inc(rstd_done, 1)

            def rotated(c, gb):
                pool.wait_ge(rot_done, gb * 4 + c + 1)
                dst = qk[:, c // 2, c % 2, :].rearrange("p (h d) -> p h d", h=RH)[:, :, 0:ROT]
                nc.gpsimd.tensor_tensor(dst, t1[:, :, :], t2[:, :, :], ALU.add).then_inc(rot_added, 1)

            def body(b, nxt, norm):
                pool.wait_ge(vh_done, b + 1)
                for e in range(2):
                    dst, hi = (a[:, :, :, e * RD:(e + 1) * RD].rearrange("p t (m e) d -> p t m e d", e=2)[:, :, :, e, :] for a in (vl, vh))
                    src = vraw[:, :, :].rearrange("p t (m e d) -> p t m e d", e=2, d=RD)[:, :, :, e, :]
                    last = nc.gpsimd.tensor_tensor(dst, src, as_f32(hi), ALU.subtract)
                last.then_inc(vl_done, 1)
                for h in range(RH):
                    pool.wait_ge(sh_done, b * 8 + h + 1)
                    nc.gpsimd.tensor_tensor(sl[:, h % 2, :], sd[:, h % 2, :], as_f32(sh[:, h % 2, :]), ALU.subtract).then_inc(sl_done, 1)
                    if h == 0:
                        pool.wait_ge(n_done, b + 1)
                        nc.gpsimd.tensor_tensor(flat(d), flat(n), two[:, :].to_broadcast([P, KT * S]), ALU.add).then_inc(d_done, 1)
                        if nxt:
                            pool.wait_ge(tk_done, b + 1)
                    if nxt and h % 2:
                        rotated(h // 2, b + 1)
                pool.wait_ge(gvar_done, b + 1)
                nc.gpsimd.tensor_tensor(gvar[:, :], gvar[:, :], power[:, :].to_broadcast([P, KT]), ALU.pow).then_inc(gpow_done, 1)
                pool.wait_ge(zh_done, b + 1)
                nc.gpsimd.tensor_tensor(zl[:, :, :], z[:, :, :], as_f32(zh[:, :, :]), ALU.subtract).then_inc(zl_done, 1)
                if norm:
                    root(b + 2)

            nc.gpsimd.memset(as_f32(vh[:, :, :, :]), 0.0).then_inc(pads, 1)
            nc.gpsimd.memset(as_f32(vl[:, :, :, :]), 0.0).then_inc(pads, 1)
            for a, value in ((two, 2.0), (power, -0.5)):
                nc.gpsimd.memset(a[:, :], value).then_inc(pads, 1)
            pool.wait_ge(pads, 4)
            pool.sem_inc(zl_done, 1)
            pool.sem_inc(sl_done, 2)
            pool.sem_inc(ret_done, 2)
            pool.sem_inc(y_done, 1)
            root(0)
            for c in range(4):
                rotated(c, 0)
            root(1)
            with pool.Fori(0, B - 2) as b:
                body(b, True, True)
            body(B - 2, True, False)
            body(B - 1, False, False)


def cross_attention(nc, X, wb_dram, ctx_dram, pos_dram, freq_dram, bout_dram, ident):
    VW = 3 * XD + 1
    TWO_PI = 2.0 * np.pi
    with ExitStack() as mem:
        def sb(name, shape, dt=FP32):
            return mem.enter_context(nc.sbuf_tensor("b_" + name, shape, dt))

        def sem(name):
            return nc.alloc_semaphore("b_" + name)

        wh, wl = sb("wh", [P, 3, 2048], FP32R), sb("wl", [P, 3, 2048], FP32R)
        qs = sb("qs", [P, 2, TB, XH * 64])
        with nc.sbuf_tensor("b_raw", [P, 3, 2048], FP32) as whole:
            raw = [whole[:, k, :] for k in range(3)]
        qT, kT = sb("qT", [P, XH // 2, S], FP32R), sb("kT", [P, XH // 2, S], FP32R)
        xn = sb("xn", [P, TB, C])
        xh, xl = sb("xh", [P, KT, S], FP32R), sb("xl", [P, KT, S], FP32R)
        craw = sb("craw", [P, CKT, S])
        ch, cl = sb("ch", [P, CKT, S], FP32R), sb("cl", [P, CKT, S], FP32R)
        pf = sb("pf", [P, 2, TB * S])
        ph, pl = sb("ph", [P, 4, TB * S], FP16), sb("pl", [P, 4, TB * S], FP16)
        vn, v3 = sb("vn", [P, TB * XH, XD]), sb("v3", [P, TB * XH, VW], BF16)
        attn = sb("attn", [P, TB, C])
        ah, al = xh, xl
        ac, bs = sb("ac", [P, 2, XH, 8]), sb("bs", [P, 2, XH, 8])
        rr = sb("rr", [P, XH, XD])
        pos, freq, bout = sb("pos", [P, NT, 2]), sb("freq", [P, 2, 4]), sb("bout", [P, C])
        ang, turns, cs = (sb(k, [P, 2, NT * 8]) for k in ("ang", "turns", "cs"))
        st, mv = sb("st", [P, TB, 6]), sb("mv", [P, TB, 2])
        var, rstd, spare, power = sb("var", [P, TB]), sb("rstd", [P, TB]), sb("spare", [P, 1]), sb("power", [P, 1])
        zero, lift = sb("zero", [P, 1]), sb("lift", [P, 1])
        mx = sb("mx", [P, TB, XH])
        nm = sb("nm", [P, TB, P])
        mT = sb("mT", [32, 2, S], FP32R)
        rs, os = sb("rs", [P, TB * 4]), sb("os", [P, TB * 4, XD])

        def pb(name, shape):
            return mem.enter_context(nc.psum_tensor("b_" + name, shape, FP32))

        rt = pb("rt", [P, 4, 512])
        av = pb("av", [P, 2, 512])
        gm = pb("gm", [P, 2, 512])

        raw_in, pos_in, ctx_in = [sem("raw_in%d" % k) for k in range(3)], sem("pos_in"), sem("ctx_in")
        presets, ang_own = sem("presets"), sem("ang_own")
        wh_done, wl_done = sem("wh_done"), sem("wl_done")
        ang_done, cs_done = sem("ang_done"), sem("cs_done")
        bn_done, var_done, rstd_done, xn_done = sem("bn_done"), sem("var_done"), sem("rstd_done"), sem("xn_done")
        ch_done, cl_done = sem("ch_done"), sem("cl_done")
        gm_mm, gm_read = [sem("gm_mm0"), sem("gm_mm1")], [sem("gm_read0"), sem("gm_read1")]
        xh_done, ah_done = sem("xh_done"), sem("ah_done")
        summed, rh_done, rl_done = sem("summed"), sem("rh_done"), sem("rl_done")
        vpart, vrest = sem("vpart"), sem("vrest")
        row_mm, mx_done, nmh_done, nm_done = sem("row_mm"), sem("mx_done"), sem("nmh_done"), sem("nm_done")
        m_moved = [sem("m_moved0"), sem("m_moved1")]
        st_mm, e_done, ph_done, pl_done, av_done, rs_done, attn_done = (
            sem(k) for k in ("st_mm", "e_done", "ph_done", "pl_done", "av_done", "rs_done", "attn_done"))
        block = mem.enter_context(nc.Block())

        T, LAGS, LAGV = 33, 13, 16
        NORM, CONTEXT, ROWS = -T, 6 - T, {0: 15 - T, 1: 18 - T, 2: 21 - T, 3: 24 - T}
        VPART = {(0, 0): 5, (0, 1): 8, (0, 2): 11, (1, 0): 16, (1, 1): 19, (1, 2): 22}
        USES = [(6 - T, "x", 0), (6 - T, "x", 1)] + [(ROWS[n], "r", n) for n in range(4)] + [(1, "v", 0), (3, "v", 1)]
        for f, step in enumerate((-5, -3, 4, 12)):
            USES += [(step + n // 2, "t", 4 * f + n) for n in range(4)]
        USES += [(9 + 8 * k, "m", k) for k in range(4)] + [(LAGV + 36, "o", t) for t in range(TB)] + [(LAGV + 38, "w", t) for t in range(TB)]
        ORDER = sorted(USES, key=lambda use: use[0] % T)
        BANK = {use[1:]: n % 2 for n, use in enumerate(ORDER)}

        def uses(g, what, n):
            place = [use[1:] for use in ORDER].index((what, n))
            ahead = ORDER[place][0] // T
            total, per = 0, 0
            for m, use in enumerate(ORDER):
                if m % 2 == place % 2:
                    more = ahead - use[0] // T + (m <= place)
                    if isinstance(g, int):
                        total += min(max(g + more, 0), B)
                    else:
                        total, per = total + more, per + 1
            return total if isinstance(g, int) else g * per + total

        def due(i, live, step):
            return [d for d in live if i - d * T == step]

        def heads(i, live, lag):
            return [(d, i - d * T - lag) for d in live if 0 <= i - d * T - lag < XH]

        def of_half(v, half):
            return v[:, :, :].rearrange("p (t h) d -> p t h d", t=TB)[:, :, 16 * half:16 * half + 16, :]

        def bodies(engine, run):
            run(-1, (1,))
            run(0, (0, 1))
            with engine.Fori(1, B - 1) as b:
                run(b, (-1, 0, 1))
            run(B - 1, (-1, 0))
            run(B, (-1,))

        def fresh(g):
            return isinstance(g, int) and g <= 0

        @block.sync
        def _(sp):
            sp.dma_start(raw[0], wb_dram[0, :, :]).then_inc(raw_in[0], 16)
            sp.dma_start(pos[:, :, :], pos_dram).then_inc(pos_in, 16)
            sp.dma_start(freq[:, :, :], freq_dram).then_inc(pos_in, 16)
            sp.dma_start(bout[:, :], bout_dram).then_inc(pos_in, 16)
            sp.dma_start(craw[:, :, :], ctx_dram[0, :, :, :]).then_inc(ctx_in, 16)
            for k in range(1, 3):
                sp.dma_start(raw[k], wb_dram[k, :, :]).then_inc(raw_in[k], 16)

            def body(b, nxt):
                if nxt:
                    sp.wait_ge(cl_done, b + 1)
                    sp.dma_start(craw[:, :, :], ctx_dram[b + 1, :, :, :]).then_inc(ctx_in, 16)
                for k in range(4):
                    sp.wait_ge(gm_read[BANK["m", k]], uses(b, "m", k))
                    for c in range(2):
                        for e in range(2):
                            row = 64 * e + 48 + c
                            sp.dma_start(as_f32(qT[row:row + 1, 4 * k:4 * k + 4, :]),
                                         as_f32(mT[8 * c + e:8 * c + e + 7:2, k % 2, :])).then_inc(m_moved[k % 2], 16)

            body(0, True)
            with sp.Fori(1, B - 1) as b:
                body(b, True)
            body(B - 1, False)

        @block.tensor
        def _(pe):
            def rows(g, h):
                if h % 8 == 0:
                    for n in (h // 2 + 2, h // 2 + 3):
                        pe.wait_ge(gm_read[BANK["t", n]], uses(g, "t", n))
                pe.wait_ge(mx_done, g * XH + (h + 1))
                r, m = 64 * (h % 2), h // 2
                for t in range(TB):
                    last = nc.tensor.matmul(rt[:, h % 2, t * S:(t + 1) * S], qT[r:r + 64, m, t * P:(t + 1) * P], kT[r:r + 64, m, :],
                                            start=True, stop=True)
                last.then_inc(row_mm, 1)

            def logits(g, h):
                k = h // 8
                if h % 8 == 0:
                    pe.wait_ge(m_moved[k % 2], g * 128 + (k // 2 * 64 + 64))
                pe.wait_ge(e_done, g * XH + (h + 1))
                r, m = 64 * (h % 2), h // 2
                for j in range(TB):
                    last = nc.tensor.matmul(rt[:, 2 + h % 2, j * S:(j + 1) * S], kT[r:r + 64, m, j * P:(j + 1) * P], qT[r:r + 64, m, :],
                                            start=True, stop=True)
                last.then_inc(st_mm, 1)

            def values(g, h):
                q = h // 4
                if h % 16 == 0:
                    pe.wait_ge(vpart, g * 6 + (h // 16 * 3 + 3))
                if h % 4 == 0:
                    pe.wait_ge(attn_done, g * 8 + (q + 1))
                pe.wait_ge(pl_done, g * XH + (h + 3))
                for t in range(TB):
                    o = (t * 4 + h % 4) * VW
                    for j in range(TB):
                        a = slice(j * S + t * P, j * S + (t + 1) * P)
                        nc.tensor.matmul(av[:, q % 2, o:o + VW], pl[:, h % 4, a], v3[:, j * XH + h, :], start=j == 0, stop=False)
                        last = nc.tensor.matmul(av[:, q % 2, o:o + VW], ph[:, h % 4, a], v3[:, j * XH + h, :],
                                                start=False, stop=j == TB - 1)
                last.then_inc(av_done, 1)

            def use(g, what, n):
                bank = BANK[what, n]
                before = uses(g, what, n) - 1
                if not (isinstance(before, int) and before == 0):
                    pe.wait_ge(gm_read[bank], before)
                out = gm[:, bank, :]
                a = slice(n % 2 * P, (n % 2 + 1) * P)
                if what == "x":
                    if n == 0:
                        pe.wait_ge(xn_done, g + 1)
                    for m in range(KT):
                        last = nc.tensor.transpose(out[:, m * P:(m + 1) * P], xn[:, n, m * P:(m + 1) * P], ident[:, :])
                elif what == "r" and n < 2:
                    if n == 0:
                        pe.wait_ge(wl_done, 1)
                    for m in range(KT):
                        last = matmul3(nc, out, (xh[:, m, a], xl[:, m, a]), (wh[:, 0, m * C:(m + 1) * C], wl[:, 0, m * C:(m + 1) * C]),
                                       m == 0, m == KT - 1)
                elif what in ("r", "v"):
                    if what == "r":
                        pe.wait_ge(wl_done, 2)
                        pe.wait_ge(cl_done, g + 1)
                    for m in range(CKT):
                        o = (2 * m + (what == "v")) * C
                        last = matmul3(nc, out, (ch[:, m, a], cl[:, m, a]), (wh[:, 1, o:o + C], wl[:, 1, o:o + C]),
                                       m == 0, m == CKT - 1)
                elif what == "t":
                    if n == 0:
                        pe.wait_ge(rl_done, g * 4 + 4)
                    f, which, t = n // 4, n // 2 % 2, n % 2
                    for m in range(4):
                        c = (f * 4 + m) * P
                        last = nc.tensor.transpose(out[:, m * P:(m + 1) * P], qs[:, which, t, c:c + P], ident[:, :])
                elif what == "m":
                    pe.wait_ge(nm_done, g * 4 + (n + 1))
                    for t in range(TB):
                        last = nc.tensor.transpose(out[:, t * P:(t + 1) * P], nm[:, t, :], ident[:, :])
                elif what == "o":
                    if n == 0:
                        pe.wait_ge(attn_done, g * 8 + 10)
                    for m in range(KT):
                        last = nc.tensor.transpose(out[:, m * P:(m + 1) * P], attn[:, n, m * P:(m + 1) * P], ident[:, :])
                else:
                    if n == 0:
                        pe.wait_ge(wl_done, 3)
                    other = "o", n
                    pe.wait_ge(gm_read[BANK[other]], uses(g, *other))
                    for m in range(KT):
                        last = matmul3(nc, out, (ah[:, m, a], al[:, m, a]), (wh[:, 2, m * C:(m + 1) * C], wl[:, 2, m * C:(m + 1) * C]),
                                       m == 0, m == KT - 1)
                last.then_inc(gm_mm[bank], 1)

            def body(b, live):
                for i in range(T):
                    for d, h in heads(i, live, 0):
                        rows(b + d, h)
                    for d, h in heads(i, live, LAGS):
                        logits(b + d, h)
                    for d, h in heads(i, live, LAGV):
                        values(b + d, h)
                    for step, what, n in ORDER:
                        for d in due(i, live, step):
                            use(b + d, what, n)

            bodies(pe, body)

        @block.vector
        def _(dve):
            def statistics(g):
                for t in range(TB):
                    last = nc.vector.bn_stats(out=st[:, t, :], in_=X[:, g * TB + t, :])
                last.then_inc(bn_done, 1)
                dve.wait_ge(bn_done, g * 2 + 1)
                nc.vector.tensor_copy(spare[:, :], st[:, 0, 0:1])
                for t in range(TB):
                    last = nc.vector.bn_aggr(out=mv[:, t, :], in_=st[:, t, :])
                last.then_inc(bn_done, 1)
                dve.wait_ge(bn_done, g * 2 + 2)
                nc.vector.tensor_scalar(var[:, :], mv[:, :, 1], EPS, None, ALU.add).then_inc(var_done, 1)

            def normalize(g):
                dve.wait_ge(rstd_done, g + 1)
                for t in range(TB):
                    last = nc.vector.tensor_scalar(xn[:, t, :], X[:, g * TB + t, :],
                                                   mv[:, t, 0:1], rstd[:, t:t + 1], ALU.subtract, ALU.mult)
                last.then_inc(xn_done, 1)

            def take(g, what, n):
                bank = BANK[what, n]
                src = gm[:, bank, :]
                a = slice(n % 2 * P, (n % 2 + 1) * P)
                if what in ("x", "o"):
                    high, low, done = (xh, xl, xh_done) if what == "x" else (ah, al, ah_done)
                    dve.wait_ge(done, g * 2 + (n + 1))
                    nc.vector.tensor_tensor(low[:, :, a], src.rearrange("p (m s) -> p m s", s=P), as_f32(high[:, :, a]), ALU.subtract)\
                        .then_inc(gm_read[bank], 1)
                elif what == "r":
                    dve.wait_ge(gm_mm[bank], uses(g, what, n))
                    if n == 0:
                        dve.wait_ge(cs_done, 1)
                    if not (fresh(g) and n == 0):
                        dve.wait_ge(summed, g * 4 + n)
                    view = src.rearrange("p (k i) -> p k i", i=8)
                    for k, dst in enumerate((ac, bs)):
                        table = cs[:, k, bass.ts(g * TB + n % 2, 8)].rearrange("p (o i) -> p o i", o=1).to_broadcast([P, 2 * XH, 8])
                        last = nc.vector.tensor_tensor(dst[:, :, :, :].rearrange("p c h i -> p (c h) i"), view, table, ALU.mult)
                    last.then_inc(gm_read[bank], 1)
                elif what == "t" and n % 2:
                    dve.wait_ge(gm_mm[bank], uses(g, what, n))
                    f, which, t = n // 4, n // 2 % 2, n % 2
                    nc.vector.tensor_copy((qT, kT)[which][:, f * 4:f * 4 + 4, a],
                                          src.rearrange("p (m s) -> p m s", s=P)).then_inc(gm_read[bank], 1)
                elif what == "w":
                    dve.wait_ge(gm_mm[bank], uses(g, what, n))
                    tile = X[:, g * TB + n, :]
                    nc.vector.tensor_tensor(tile, src, tile, ALU.add).then_inc(gm_read[bank], 1)
                    dve.wait_ge(gm_read[bank], uses(g, what, n))
                    nc.vector.tensor_tensor(tile, tile, bout[:, :], ALU.add)

            def maximum(g, h):
                dve.wait_ge(row_mm, g * XH + (h + 1))
                nc.vector.tensor_reduce(out=mx[:, :, h], in_=rt[:, h % 2, :].rearrange("p (t s) -> p t s", s=S),
                                        op=ALU.max, axis=AX.X).then_inc(mx_done, 1)

            def negate(g, k):
                dve.wait_ge(mx_done, g * XH + (8 * k + 10))
                part = mx[:, :, 8 * k:8 * k + 8]
                if not (fresh(g) and k == 0):
                    other = ("m", (k - 1) % 4)
                    dve.wait_ge(gm_read[BANK[other]], uses(g if k else g - 1, *other))
                else:
                    dve.wait_ge(presets, 8)
                nc.vector.tensor_scalar(nm[:, :, 0:8].bitcast(FP32R), part, -1.0, None, ALU.mult).then_inc(nmh_done, 1)
                dve.wait_ge(nmh_done, g * 4 + (k + 1))
                nc.vector.scalar_tensor_tensor(out=nm[:, :, 8:16], in0=part, scalar=-1.0, in1=nm[:, :, 0:8],
                                               op0=ALU.mult, op1=ALU.subtract).then_inc(nm_done, 1)

            def high_exp(g, h):
                dve.wait_ge(e_done, g * XH + (h + 3))
                dve.wait_ge(av_done, g * XH + (h + 1))
                nc.vector.tensor_copy(ph[:, h % 4, :], pf[:, h % 2, :]).then_inc(ph_done, 1)

            def group(g, q):
                dve.wait_ge(attn_done, g * 8 + (q + 2))
                dve.wait_ge(av_done, g * XH + (4 * q + 8))
                src = av[:, q % 2, 0:TB * 4 * VW].rearrange("p (q d) -> p q d", d=VW)
                nc.vector.tensor_reduce(out=os[:, :, :], in_=src[:, :, 0:3 * XD].rearrange("p q (s d) -> p q d s", s=3),
                                        op=ALU.add, axis=AX.X)
                nc.vector.reciprocal(rs[:, :], src[:, :, 3 * XD]).then_inc(rs_done, 1)
                dve.wait_ge(rs_done, g * 8 + (q + 1))
                dst = attn[:, :, 64 * q:64 * q + 64].rearrange("p t (h d) -> p t h d", h=4)
                nc.vector.tensor_tensor(dst, os[:, :, :].rearrange("p (t h) d -> p t h d", t=TB),
                                        rs[:, :].rearrange("p (t h o) -> p t h o", t=TB, o=1).to_broadcast([P, TB, 4, XD]),
                                        ALU.mult).then_inc(attn_done, 1)

            def body(b, live):
                for i in range(T):
                    if isinstance(b, int) and b < 0 and i in (8, 9, 10):
                        low_weights(i - 8)
                    if isinstance(b, int) and b < 0 and i == 11:
                        angles()
                    for d in due(i, live, NORM):
                        statistics(b + d)
                    for d in due(i, live, NORM + 3):
                        normalize(b + d)
                    for step, what, n in ORDER:
                        for d in due(i, live, step + 1):
                            take(b + d, what, n)
                    for d, h in heads(i, live, 0):
                        maximum(b + d, h)
                    for k in range(4):
                        for d in due(i, live, 8 * k + 8):
                            negate(b + d, k)
                    for d, h in heads(i, live, LAGS):
                        high_exp(b + d, h)
                    for q in range(8):
                        for d in due(i, live, LAGV + 4 * q + 4):
                            group(b + d, q)

            def angles():
                own = Chain(dve, ang_own)
                dve.wait_ge(pos_in, 48)
                an = ang[:, 1, :].rearrange("p (t a i) -> p t a i", a=2, i=4)
                fr = freq[:, :, :].rearrange("p (o a) i -> p o a i", o=1).to_broadcast([P, NT, 2, 4])
                ps = pos[:, :, :].rearrange("p t (a o) -> p t a o", o=1).to_broadcast([P, NT, 2, 4])
                own.step(nc.vector.tensor_tensor(an, ps, fr, ALU.mult))
                own.step(nc.vector.tensor_scalar(ang[:, 0, :], ang[:, 1, :], float(np.pi / 2), None, ALU.add))
                ROUND = 1.5 * 2.0 ** 23
                own.step(nc.vector.tensor_scalar(turns[:, :, :], ang[:, :, :], 1.0 / TWO_PI, ROUND, ALU.mult, ALU.add))
                own.step(nc.vector.tensor_scalar(turns[:, :, :], turns[:, :, :], -ROUND, None, ALU.add))
                for part in (6.28125, TWO_PI - 6.28125):
                    own.step(nc.vector.scalar_tensor_tensor(out=ang[:, :, :], in0=turns[:, :, :], scalar=-part, in1=ang[:, :, :],
                                                            op0=ALU.mult, op1=ALU.add))
                nc.vector.tensor_scalar(ang[:, :, :], ang[:, :, :], 3.1415925, -3.1415925, ALU.min, ALU.max).then_inc(ang_done, 1)

            def low_weights(k):
                dve.wait_ge(wh_done, k + 1)
                nc.vector.tensor_tensor(wl[:, k, :], raw[k], as_f32(wh[:, k, :]), ALU.subtract).then_inc(wl_done, 1)

            dve.sem_inc(mx_done, 2)
            bodies(dve, body)

        @block.scalar
        def _(act):
            def take(g, what, n):
                bank = BANK[what, n]
                src = gm[:, bank, :]
                a = slice(n % 2 * P, (n % 2 + 1) * P)
                if what in ("x", "o", "v", "m") or (what == "t" and n % 2 == 0):
                    act.wait_ge(gm_mm[bank], uses(g, what, n))
                if what == "x":
                    if n == 0 and not (isinstance(g, int) and g < 3):
                        for t in range(TB):
                            act.wait_ge(gm_mm[BANK["w", t]], uses(g - 3, "w", t))
                    nc.scalar.copy(xh[:, :, a], src.rearrange("p (m s) -> p m s", s=P)).then_inc(xh_done, 1)
                elif what == "o":
                    if n == 0 and not (isinstance(g, int) and g + 2 >= B):
                        for t in range(TB):
                            act.wait_ge(gm_mm[BANK["r", t]], uses(g + 2, "r", t))
                    nc.scalar.copy(ah[:, :, a], src.rearrange("p (m s) -> p m s", s=P)).then_inc(ah_done, 1)
                elif what == "v":
                    if not (fresh(g)):
                        act.wait_ge(vpart, g * 6)
                    nc.scalar.copy(vn[:, n * XH:(n + 1) * XH, :].rearrange("p h d -> p (h d)"), src).then_inc(gm_read[bank], 1)
                elif what == "m":
                    if not (fresh(g) and n < 2):
                        act.wait_ge(m_moved[n % 2], g * 128 + n // 2 * 64)
                    nc.scalar.copy(mT[:, n % 2, :], src[0:32, 0:S]).then_inc(gm_read[bank], 1)
                elif what == "t" and n % 2 == 0:
                    if fresh(g) and n == 0:
                        act.wait_ge(wl_done, 3)
                    f, which = n // 4, n // 2 % 2
                    nc.scalar.copy((qT, kT)[which][:, f * 4:f * 4 + 4, a],
                                   src.rearrange("p (m s) -> p m s", s=P)).then_inc(gm_read[bank], 1)

            def high_context(g):
                act.wait_ge(ctx_in, g * 16 + 16)
                nc.scalar.copy(ch[:, :, :], craw[:, :, :]).then_inc(ch_done, 1)

            def high_rows(g, n):
                if n == 0:
                    if fresh(g):
                        act.wait_ge(presets, 8)
                    else:
                        for other in (14, 15):
                            act.wait_ge(gm_mm[BANK["t", other]], uses(g - 1, "t", other))
                act.wait_ge(summed, g * 4 + (n + 1))
                which, t = n // 2, n % 2
                apart = 32 if which == 0 else 16
                head = qs[:, which, t, :].rearrange("p (h d) -> p h d", h=XH)
                for k in range(2):
                    last = nc.scalar.copy(head[:, :, k * apart:k * apart + XD].bitcast(FP32R), rr[:, :, :])
                last.then_inc(rh_done, 1)

            def v_part(g, half, k):
                if k == 0:
                    if not fresh(g):
                        act.wait_ge(av_done, g * XH + (16 * half - 12))
                    if half == 0:
                        for t in range(TB):
                            act.wait_ge(gm_read[BANK["v", t]], uses(g, "v", t))
                else:
                    act.wait_ge(vrest, g * 4 + (2 * half + k))
                nc.scalar.copy(of_half(v3, half)[:, :, :, k * XD:(k + 1) * XD], of_half(vn, half)).then_inc(vpart, 1)

            def exponentials(g, h):
                act.wait_ge(st_mm, g * XH + (h + 1))
                act.wait_ge(pl_done, g * XH + (h + 1))
                nc.scalar.activation(pf[:, h % 2, :], rt[:, 2 + h % 2, :], ACT.Exp, scale=XD ** -0.5,
                                     bias=lift[:, :]).then_inc(e_done, 1)

            def body(b, live):
                for i in range(T):
                    if isinstance(b, int) and b < 0 and i in (6, 8, 9):
                        k = (6, 8, 9).index(i)
                        act.wait_ge(raw_in[k], 16)
                        nc.scalar.copy(wh[:, k, :], raw[k]).then_inc(wh_done, 1)
                    if isinstance(b, int) and b < 0 and i == 12:
                        act.wait_ge(ang_done, 1)
                        nc.scalar.activation(cs[:, :, :], ang[:, :, :], ACT.Sin).then_inc(cs_done, 1)
                    for step, what, n in ORDER:
                        for d in due(i, live, step + 1):
                            take(b + d, what, n)
                    for d in due(i, live, CONTEXT):
                        high_context(b + d)
                    for (half, k), step in VPART.items():
                        for d in due(i, live, step):
                            v_part(b + d, half, k)
                    for n, step in ROWS.items():
                        for d in due(i, live, step + 2):
                            high_rows(b + d, n)
                    for d, h in heads(i, live, LAGS):
                        exponentials(b + d, h)

            act.wait_ge(presets, 3)
            bodies(act, body)

        @block.gpsimd
        def _(pool):
            def root(g):
                pool.wait_ge(var_done, g + 1)
                nc.gpsimd.tensor_tensor(rstd[:, :], var[:, :], power[:, :].to_broadcast([P, TB]), ALU.pow).then_inc(rstd_done, 1)

            def low_context(g):
                pool.wait_ge(ch_done, g + 1)
                nc.gpsimd.tensor_tensor(cl[:, :, :], craw[:, :, :], as_f32(ch[:, :, :]), ALU.subtract).then_inc(cl_done, 1)

            def sum_rows(g, n):
                pool.wait_ge(gm_read[BANK["r", n]], uses(g, "r", n))
                if not (fresh(g) and n == 0):
                    pool.wait_ge(rl_done, g * 4 + n)
                nc.gpsimd.tensor_tensor(rr[:, :, 0:8], ac[:, 0, :, :], bs[:, 1, :, :], ALU.subtract)
                nc.gpsimd.tensor_tensor(rr[:, :, 8:16], bs[:, 0, :, :], ac[:, 1, :, :], ALU.add).then_inc(summed, 1)

            def low_rows(g, n):
                pool.wait_ge(rh_done, g * 4 + (n + 1))
                which, t = n // 2, n % 2
                o = 16 if which == 0 else 32
                head = qs[:, which, t, :].rearrange("p (h d) -> p h d", h=XH)
                nc.gpsimd.tensor_tensor(head[:, :, o:o + XD], rr[:, :, :], head[:, :, 0:XD], ALU.subtract).then_inc(rl_done, 1)

            def v_rest(g, half, k):
                pool.wait_ge(vpart, g * 6 + (3 * half + k + 1))
                v = of_half(vn, half)
                nc.gpsimd.tensor_tensor(v, v, of_half(v3, half)[:, :, :, k * XD:(k + 1) * XD], ALU.subtract).then_inc(vrest, 1)

            def low_exp(g, h):
                pool.wait_ge(ph_done, g * XH + (h + 1))
                nc.gpsimd.tensor_tensor(pl[:, h % 4, :], pf[:, h % 2, :], ph[:, h % 4, :], ALU.subtract).then_inc(pl_done, 1)

            def body(b, live):
                for i in range(T):
                    if isinstance(b, int) and b < 0 and i == 8:
                        clear_rows()
                    for d in due(i, live, NORM + 1):
                        root(b + d)
                    for d in due(i, live, CONTEXT + 1):
                        low_context(b + d)
                    for n, step in ROWS.items():
                        for d in due(i, live, step + 2):
                            low_rows(b + d, n)
                        for d in due(i, live, step + 1):
                            sum_rows(b + d, n)
                    for (half, k), step in VPART.items():
                        if k < 2:
                            for d in due(i, live, step + 1):
                                v_rest(b + d, half, k)
                    for d, h in heads(i, live, LAGS):
                        low_exp(b + d, h)

            def clear_rows():
                nc.gpsimd.memset(v3[:, :, :], 1.0).then_inc(presets, 1)
                nc.gpsimd.memset(nm[:, :, :], 0.0).then_inc(presets, 1)
                nc.gpsimd.memset(qs[:, 0, :, :], 0.0).then_inc(presets, 1)
                nc.gpsimd.memset(qs[:, 1, :, :], 0.0).then_inc(presets, 1)
                pool.wait_ge(presets, 7)
                nc.gpsimd.memset(qs[:, 1, :, :].rearrange("p t (h d) -> p (t h) d", d=64)[:, :, 48:50], 1.0).then_inc(presets, 1)

            nc.gpsimd.memset(power[:, :], -0.5).then_inc(presets, 1)
            nc.gpsimd.memset(zero[:, :], 0.0).then_inc(presets, 1)
            nc.gpsimd.memset(lift[:, :], float(11 * np.log(2.0))).then_inc(presets, 1)
            pool.wait_ge(presets, 3)
            pool.sem_inc(pl_done, 2)
            pool.sem_inc(e_done, 2)
            pool.sem_inc(av_done, 4)
            pool.sem_inc(attn_done, 2)
            bodies(pool, body)


def feed_forward(nc, X, wc_dram, sel_dram, gate_dram, key_dram, ident, out_dram):
    G = NT // 4
    PW = 3 * C
    with ExitStack() as mem:
        def sb(name, shape, dt=FP32):
            return mem.enter_context(nc.sbuf_tensor("c_" + name, shape, dt))

        def pb(name, shape, stack):
            return stack.enter_context(nc.psum_tensor("c_" + name, shape, FP32))

        def sem(name):
            return nc.alloc_semaphore("c_" + name)

        xh, xl = sb("xh", [P, KT, NT * P], FP32R), sb("xl", [P, KT, NT * P], FP32R)
        raw, sraw = sb("raw", [P, 2, PW]), sb("sraw", [32, 2, P])
        wh, wl = sb("wh", [P, 4, PW], FP32R), sb("wl", [P, 4, PW], FP32R)
        sel = sb("sel", [32, 4, P], FP32R)
        cT = sb("cT", [32, NT * P], FP32R)
        with nc.sbuf_tensor("c_xn", [P, 4, C], FP32) as xn:
            pass
        with nc.sbuf_tensor("c_cc", [P, NT, P], FP32) as cc:
            pass
        hh = sb("hh", [P, 4, C], FP32R)
        hl = sb("hl", [P, 4, C], FP32R)
        s, t, hf = sb("s", [P, 2, C]), sb("t", [P, C]), sb("hf", [P, 2, C])
        st, mv = sb("st", [P, 4, 6]), sb("mv", [P, 4, 2])
        var, rstd, spare, power = sb("var", [P, 4]), sb("rstd", [P, 4]), sb("spare", [P, 1]), sb("power", [P, 1])
        zero = sb("zero", [P, 1])
        graw = sb("graw", [P, KT, P])
        gwh, gwl = sb("gwh", [P, KT, P], FP32R), sb("gwl", [P, KT, P], FP32R)
        lg = sb("lg", [P, C])
        L = sb("L", [P, NT, 16])
        key = sb("key", [P, E])
        prob, work, chosen, hit = (sb(k, [P, NT, E]) for k in ("prob", "work", "chosen", "hit"))
        top, den = sb("top", [P, NT]), sb("den", [P, NT])
        shared = sb("shared", [P, NT])

        with ExitStack() as early:
            tp = pb("tp", [P, 4, C], early)
            rl, rt = pb("rl", [P, C], early), pb("rt", [P, 4, P], early)
        fc = pb("fc", [P, 2, 2, C], mem)
        with ExitStack() as early:
            ct = pb("ct", [P, 4, C], early)
        gate = pb("gate", [P, C], mem)
        yp = pb("yp", [P, 3, C], mem)

        raw_in, sraw_in = [sem("raw_in0"), sem("raw_in1")], [sem("sraw_in0"), sem("sraw_in1")]
        const_in, out_done = sem("const_in"), sem("out_done")
        own_sem = sem("dve_own")
        var_done, rstd_done, xn_done, power_set = sem("var_done"), sem("rstd_done"), sem("xn_done"), sem("power_set")
        tx_done, xh_done, xl_done = sem("tx_done"), sem("xh_done"), sem("xl_done")
        gwh_done, gwl_done = sem("gwh_done"), sem("gwl_done")
        rl_done, lg_done, rt_done, L_done = sem("rl_done"), sem("lg_done"), sem("rt_done"), sem("L_done")
        shifted, exp_done, cc_done, ct_t, ct_done = sem("shifted"), sem("exp_done"), sem("cc_done"), sem("ct_t"), sem("ct_done")
        wh_done, w_done = sem("wh_done"), sem("w_done")
        fc_done, s_done, t_done, hf_done, hh_done, hl_done = (sem(k) for k in ("fc_done", "s_done", "t_done", "hf_done", "hh_done", "hl_done"))
        ymm_done, added = sem("ymm_done"), sem("added")
        CH = FT // 2
        TURNS = CH // 2
        LAST = 2 * G * CH
        block = mem.enter_context(nc.Block())

        @block.sync
        def _(sp):
            def piece(f, slot, used):
                if used is not None:
                    sp.wait_ge(w_done, used)
                sp.dma_start(raw[:, slot, :], wc_dram[f, :, :]).then_inc(raw_in[slot], 16)
                sp.dma_start(sraw[:, slot, :], sel_dram[f, :, :]).then_inc(sraw_in[slot], 16)

            sp.dma_start(graw[:, :, :], gate_dram).then_inc(const_in, 16)
            sp.dma_start(key[:, :], key_dram).then_inc(const_in, 16)
            for f in range(4):
                piece(f, f % 2, f - 1 if f >= 2 else None)
            with sp.Fori(0, TURNS - 1) as it:
                for k in range(4):
                    piece(it * 4 + (4 + k), k % 2, it * 4 + (3 + k))
            piece(FT - 1, 0, FT - 2)
            for g in range(G):
                sp.wait_ge(added, (CH * G + g) * 4 + 5)
                sp.dma_start(out_dram[:, 4 * g:4 * g + 4, :], X[:, 4 * g:4 * g + 4, :]).then_inc(out_done, 16)
            sp.wait_ge(out_done, 16 * G)

        @block.gpsimd
        def _(pool):
            def split(f, slot, wslot, raws, used):
                pool.wait_ge(raw_in[slot], raws)
                pool.wait_ge(sraw_in[slot], raws)
                if used is not None:
                    pool.wait_ge(ymm_done, used * 4)
                nc.gpsimd.tensor_tensor(wh[:, wslot, :], raw[:, slot, :], zero[:, :].to_broadcast([P, PW]), ALU.add)
                nc.gpsimd.tensor_tensor(sel[:, wslot, :], sraw[:, slot, :], zero[0:32, :].to_broadcast([32, P]), ALU.add)\
                    .then_inc(wh_done, 1)
                pool.wait_ge(wh_done, f + 1)
                nc.gpsimd.tensor_tensor(wl[:, wslot, :], raw[:, slot, :], as_f32(wh[:, wslot, :]), ALU.subtract)\
                    .then_inc(w_done, 1)

            nc.gpsimd.memset(power[:, :], -0.5).then_inc(power_set, 1)
            nc.gpsimd.memset(zero[:, :], 0.0).then_inc(power_set, 1)
            pool.wait_ge(power_set, 2)
            for g in range(G):
                pool.wait_ge(var_done, g + 1)
                nc.gpsimd.tensor_tensor(rstd[:, :], var[:, :], power[:, :].to_broadcast([P, 4]), ALU.pow).then_inc(rstd_done, 1)
                if g == G - 1:
                    for f in range(4):
                        split(f, f % 2, f, 16 * (f // 2 + 1), None)
            with pool.Fori(0, TURNS - 1) as it:
                for k in range(4):
                    split(it * 4 + (4 + k), k % 2, k, it * 32 + (3 + k // 2) * 16, it * 8 + (6 + 4 * (k // 2)))
            split(FT - 1, 0, 0, (FT // 2 + 1) * 16, (CH - 2) * G + 6)

        @block.vector
        def _(dve):
            own = Chain(dve, own_sem)
            dve.sem_inc(xl_done, 4)
            dve.sem_inc(t_done, 1)
            dve.sem_inc(added, 1)
            dve.sem_inc(ymm_done, 8)

            def statistics(g):
                for k in range(4):
                    last = nc.vector.bn_stats(out=st[:, k, :], in_=X[:, g * 4 + k, :])
                own.step(last)
                nc.vector.tensor_copy(spare[:, :], st[:, 0, 0:1])
                for k in range(4):
                    last = nc.vector.bn_aggr(out=mv[:, k, :], in_=st[:, k, :])
                own.step(last)
                nc.vector.tensor_scalar(var[:, :], mv[:, :, 1], EPS, None, ALU.add).then_inc(var_done, 1)

            def normalize(g):
                dve.wait_ge(rstd_done, g + 1)
                for k in range(4):
                    if g:
                        dve.wait_ge(tx_done, g * 4 + (k - 3))
                    nc.vector.tensor_scalar(xn[:, k, :], X[:, g * 4 + k, :], mv[:, k, 0:1], rstd[:, k:k + 1],
                                            ALU.subtract, ALU.mult).then_inc(xn_done, 1)

            def low_x(g):
                for k in range(4):
                    dve.wait_ge(xh_done, g * 4 + (k + 1))
                    at = slice((g * 4 + k) * P, (g * 4 + k + 1) * P)
                    nc.vector.tensor_tensor(xl[:, :, at], tp[:, k, :].rearrange("p (m s) -> p m s", s=P), as_f32(xh[:, :, at]),
                                            ALU.subtract).then_inc(xl_done, 1)

            def router_logits(g):
                dve.wait_ge(rt_done, g + 1)
                nc.vector.tensor_copy(L[:, 4 * g:4 * g + 4, :], rt[:, :, 0:16]).then_inc(L_done, 1)

            statistics(0)
            normalize(0)
            statistics(1)
            dve.wait_ge(gwh_done, 1)
            nc.vector.tensor_tensor(gwl[:, :, :], graw[:, :, :], as_f32(gwh[:, :, :]), ALU.subtract).then_inc(gwl_done, 1)
            for g in range(G):
                if g + 1 < G:
                    normalize(g + 1)
                low_x(g)
                if g + 2 < G:
                    statistics(g + 2)
                if g > 1:
                    router_logits(g - 2)
            router_logits(G - 2)
            router_logits(G - 1)
            dve.wait_ge(const_in, 32)

            def wide(a):
                return a[:, :].rearrange("p (t o) -> p t o", o=1).to_broadcast([P, NT, E])

            dve.wait_ge(L_done, G)
            own.step(nc.vector.tensor_reduce(out=top[:, :], in_=L[:, :, 0:E], op=ALU.max, axis=AX.X))
            nc.vector.tensor_tensor(prob[:, :, :], L[:, :, 0:E], wide(top), ALU.subtract).then_inc(shifted, 1)
            dve.wait_ge(exp_done, 1)
            own.step(nc.vector.tensor_reduce(out=den[:, :], in_=prob[:, :, :], op=ALU.add, axis=AX.X))
            own.step(nc.vector.reciprocal(den[:, :], den[:, :]))
            own.step(nc.vector.tensor_tensor(prob[:, :, :], prob[:, :, :], wide(den), ALU.mult))
            keys = key[:, :].rearrange("p (o e) -> p o e", o=1).to_broadcast([P, NT, E])
            own.step(nc.vector.tensor_copy(work[:, :, :], prob[:, :, :]))
            for k in range(2):
                own.step(nc.vector.tensor_reduce(out=top[:, :], in_=work[:, :, :], op=ALU.max, axis=AX.X))
                own.step(nc.vector.tensor_tensor(hit[:, :, :], work[:, :, :], wide(top), ALU.is_equal))
                own.step(nc.vector.tensor_tensor(hit[:, :, :], hit[:, :, :], keys, ALU.mult))
                own.step(nc.vector.tensor_reduce(out=top[:, :], in_=hit[:, :, :], op=ALU.max, axis=AX.X))
                mark = chosen if k == 0 else hit
                own.step(nc.vector.tensor_tensor(mark[:, :, :], hit[:, :, :], wide(top), ALU.is_equal))
                if k == 0:
                    own.step(nc.vector.scalar_tensor_tensor(out=work[:, :, :], in0=chosen[:, :, :], scalar=-2.0, in1=prob[:, :, :],
                                                            op0=ALU.mult, op1=ALU.add))
            own.step(nc.vector.tensor_tensor(chosen[:, :, :], chosen[:, :, :], hit[:, :, :], ALU.add))
            own.step(nc.vector.tensor_tensor(prob[:, :, :], prob[:, :, :], chosen[:, :, :], ALU.mult))
            own.step(nc.vector.tensor_scalar(shared[:, :], shared[:, :], 1.0, None, ALU.add))
            own.step(nc.vector.reciprocal(shared[:, :], shared[:, :]))
            own.step(nc.vector.memset(cc[:, :, :], 0.0))
            hi = cc[:, :, 0:GATES].bitcast(FP32R)
            nc.vector.tensor_copy(hi[:, :, 0:E], prob[:, :, :])
            own.step(nc.vector.tensor_copy(hi[:, :, E:GATES].rearrange("p t o -> p (t o)"), shared[:, :]))
            nc.vector.tensor_tensor(cc[:, :, 16:16 + E], prob[:, :, :], cc[:, :, 0:E], ALU.subtract)
            nc.vector.tensor_tensor(cc[:, :, 16 + E:16 + GATES].rearrange("p t o -> p (t o)"), shared[:, :],
                                    cc[:, :, E:GATES].rearrange("p t o -> p (t o)"), ALU.subtract).then_inc(cc_done, 1)
            dve.wait_ge(ct_t, 1)
            nc.vector.tensor_copy(cT[:, :], ct[0:32, :, :].rearrange("p k c -> p (k c)")).then_inc(ct_done, 1)

            def hidden(n, par):
                dve.wait_ge(s_done, n + 1)
                nc.vector.tensor_tensor(t[:, :], s[:, par, :], fc[:, par, 1, :], ALU.mult).then_inc(t_done, 1)
                dve.wait_ge(t_done, n + 2)
                nc.vector.tensor_tensor(hf[:, par, :], t[:, :], gate[:, :], ALU.mult).then_inc(hf_done, 1)

            def low(n, par, slot):
                dve.wait_ge(hh_done, n + 1)
                nc.vector.tensor_tensor(hl[:, slot, :], hf[:, par, :], as_f32(hh[:, slot, :]), ALU.subtract).then_inc(hl_done, 1)

            def add(q, g, k):
                dve.wait_ge(ymm_done, q * 4 + (k + 9))
                tile = X[:, 4 * g + k, :]
                nc.vector.tensor_tensor(tile, tile, yp[:, k % 3, :], ALU.add).then_inc(added, 1)

            hidden(0, 0)
            low(0, 0, 0)
            with dve.Fori(0, TURNS) as it:
                for qq in range(2 * G):
                    q = it * (2 * G) + qq
                    hidden(q * 2 + 1, 1)
                    low(q * 2 + 1, 1, (2 * qq + 1) % 4)
                    hidden(q * 2 + 2, 0)
                    add(q, qq % G, 0)
                    low(q * 2 + 2, 0, (2 * qq + 2) % 4)
                    for k in range(1, 4):
                        add(q, qq % G, k)
            for g in range(G):
                n = LAST + g
                if g:
                    hidden(n, n % 2)
                    low(n, n % 2, n % 4)
                    for k in range(4):
                        add(CH * G + g - 1, g - 1, k)
            for k in range(4):
                add(CH * G + G - 1, G - 1, k)

        @block.scalar
        def _(act):
            act.wait_ge(const_in, 32)
            nc.scalar.copy(gwh[:, :, :], graw[:, :, :]).then_inc(gwh_done, 1)

            def high_x(g):
                for k in range(4):
                    act.wait_ge(tx_done, g * 4 + (k + 1))
                    at = slice((g * 4 + k) * P, (g * 4 + k + 1) * P)
                    nc.scalar.copy(xh[:, :, at], tp[:, k, :].rearrange("p (m s) -> p m s", s=P)).then_inc(xh_done, 1)

            high_x(0)
            for g in range(G):
                if g + 1 < G:
                    high_x(g + 1)
                act.wait_ge(rl_done, g + 1)
                if g:
                    act.wait_ge(rt_done, g)
                nc.scalar.copy(lg[:, :], rl[:, :]).then_inc(lg_done, 1)
            act.wait_ge(shifted, 1)
            act.wait_ge(L_done, G)
            nc.scalar.activation(prob[:, :, :], prob[:, :, :], ACT.Exp)
            nc.scalar.activation(shared[:, :], L[:, :, E], ACT.Exp, scale=-1.0).then_inc(exp_done, 1)

            def silu(n, par):
                act.wait_ge(fc_done, n + 1)
                if not (isinstance(n, int) and n < 2):
                    act.wait_ge(t_done, n)
                nc.scalar.activation(s[:, par, :], fc[:, par, 0, :], ACT.Silu).then_inc(s_done, 1)

            def high(n, par, slot, used):
                act.wait_ge(hf_done, n + 1)
                act.wait_ge(ymm_done, used * 4)
                nc.scalar.copy(hh[:, slot, :], hf[:, par, :]).then_inc(hh_done, 1)

            silu(0, 0)
            high(0, 0, 0, 1)
            with act.Fori(0, TURNS) as it:
                for qq in range(2 * G):
                    q = it * (2 * G) + qq
                    silu(q * 2 + 1, 1)
                    high(q * 2 + 1, 1, (2 * qq + 1) % 4, q + 1)
                    silu(q * 2 + 2, 0)
                    high(q * 2 + 2, 0, (2 * qq + 2) % 4, q + 2)
            for n in range(LAST + 1, LAST + G):
                silu(n, n % 2)
                high(n, n % 2, n % 4, n // 2 + 1)

        @block.tensor
        def _(pe):
            def transpose_x(g):
                for k in range(4):
                    pe.wait_ge(xn_done, g * 4 + (k + 1))
                    pe.wait_ge(xl_done, g * 4 + (k + 1))
                    for m in range(KT):
                        last = nc.tensor.transpose(tp[:, k, m * P:(m + 1) * P], xn[:, k, m * P:(m + 1) * P], ident[:, :])
                    last.then_inc(tx_done, 1)

            def router(g):
                if g == 0:
                    pe.wait_ge(gwl_done, 1)
                else:
                    pe.wait_ge(lg_done, g)
                pe.wait_ge(xl_done, g * 4 + 8)
                at = slice(g * C, (g + 1) * C)
                for m in range(KT):
                    last = matmul3(nc, rl[:, :], (gwh[:, m, :], gwl[:, m, :]), (xh[:, m, at], xl[:, m, at]), m == 0, m == KT - 1)
                last.then_inc(rl_done, 1)

            def transpose_logits(g):
                pe.wait_ge(lg_done, g + 1)
                if g:
                    pe.wait_ge(L_done, g)
                for k in range(4):
                    last = nc.tensor.transpose(rt[:, k, :], lg[:, k * P:(k + 1) * P], ident[:, :])
                last.then_inc(rt_done, 1)

            transpose_x(0)
            for g in range(G):
                if g + 1 < G:
                    transpose_x(g + 1)
                router(g)
                if g:
                    transpose_logits(g - 1)
            transpose_logits(G - 1)

            def products(n, par, g, slot, pieces):
                hidden_products(n, par, g, slot, pieces)
                gates(n, g, slot)

            def hidden_products(n, par, g, slot, pieces):
                if pieces is not None:
                    pe.wait_ge(w_done, pieces)
                if not (isinstance(n, int) and n < 2):
                    pe.wait_ge(t_done, n)
                at = slice(g * C, (g + 1) * C)
                for half in range(2):
                    for m in range(KT):
                        o = half * C + m * P
                        matmul3(nc, fc[:, par, half, :], (wh[:, slot, o:o + P], wl[:, slot, o:o + P]),
                                (xh[:, m, at], xl[:, m, at]), m == 0, m == KT - 1)

            def gates(n, g, slot):
                at = slice(g * C, (g + 1) * C)
                if not (isinstance(n, int) and n == 0):
                    pe.wait_ge(hf_done, n)
                nc.tensor.matmul(gate[:, :], sel[:, slot, :], cT[:, at], start=True, stop=True).then_inc(fc_done, 1)

            def project(q, units, slots, wslots):
                pe.wait_ge(hl_done, units)
                for k in range(4):
                    if k == 0:
                        pe.wait_ge(added, q * 4 + 1)
                    if k == 3:
                        pe.wait_ge(added, q * 4 + 2)
                    for i, (hs, ws) in enumerate(zip(slots, wslots)):
                        a = slice(k * P, (k + 1) * P)
                        last = matmul3(nc, yp[:, k % 3, :], (hh[:, hs, a], hl[:, hs, a]),
                                       (wh[:, ws, 2 * C:PW], wl[:, ws, 2 * C:PW]), i == 0, i == len(slots) - 1)
                    last.then_inc(ymm_done, 1)

            hidden_products(0, 0, 0, 0, 1)
            pe.wait_ge(cc_done, 1)
            for k in range(NT):
                last = nc.tensor.transpose(ct[:, k // 4, (k % 4) * P:(k % 4 + 1) * P], cc[:, k, :], ident[:, :])
            last.then_inc(ct_t, 1)
            pe.wait_ge(ct_done, 1)
            gates(0, 0, 0)
            with pe.Fori(0, TURNS) as it:
                for qq in range(2 * G):
                    q = it * (2 * G) + qq
                    c = qq // G
                    products(q * 2 + 1, 1, qq % G, 2 * c + 1, it * 4 + (2 * c + 2) if qq % G == 0 else None)
                    nxt = (qq + 1) // G
                    products(q * 2 + 2, 0, (qq + 1) % G, (2 * nxt) % 4, it * 4 + (2 * nxt + 1) if (qq + 1) % G == 0 else None)
                    project(q, q * 2 + 2, ((2 * qq) % 4, (2 * qq + 1) % 4), (2 * c, 2 * c + 1))
            for g in range(1, G):
                products(LAST + g, g % 2, g, 0, None)
                project(CH * G + g - 1, LAST + g, ((LAST + g - 1) % 4,), (0,))
            project(CH * G + G - 1, LAST + G, ((LAST + G - 1) % 4,), (0,))


PAIRED = [2 * i + c for c in range(2) for i in range(ROT // 2)] + list(range(ROT, RD))


def retention_tables():
    j = np.arange(P)[:, None]
    near = np.concatenate([np.arange(S)[None, :] - j, np.arange(P)[None, :] - j], 1)
    gamma = 1.0 - 2.0 ** (-5.0 - np.arange(RH, dtype=np.float64))
    decay = np.where(near[:, None, :] >= 0, gamma[None, :, None] ** np.maximum(near, 0)[:, None, :], 0.0)
    t = np.arange(S, dtype=np.float32)
    inv = (np.float32(1.0) / np.float32(10000.0) ** (np.arange(0, ROT, 2, dtype=np.float32) / np.float32(ROT))).astype(np.float32)
    angle = np.repeat((t[:, None] * inv[None, :]).astype(np.float32), 2, -1).astype(np.float64)
    base = (np.arange(0, ROT, 2) + 0.4 * ROT) / (1.4 * ROT)
    scale = base[None, :] ** ((t.astype(np.float64) - S // 2) / 512.0)[:, None]
    scale = np.concatenate([scale, scale], -1)
    sign = np.where(np.arange(ROT) % 2 == 0, -1.0, 1.0)
    rot = np.stack([np.stack([np.cos(angle) * s, np.sin(angle) * s * sign]) for s in (scale, 1.0 / scale)])
    rot = rot[..., PAIRED[:ROT]].reshape(2, 2, TB, P, ROT).transpose(3, 2, 0, 1, 4)
    return decay.astype(np.float32), np.ascontiguousarray(rot.astype(np.float32))


def tiles(w):
    return w.reshape(-1, P, w.shape[1]).transpose(1, 0, 2)


def layout_retention(i):
    qkv = i["L0_attn_wqkv"].T.reshape(C, RH, 3, RD)
    q, k, v = qkv[:, :, 0][..., PAIRED], qkv[:, :, 1][..., PAIRED], qkv[:, :, 2]
    w = np.concatenate([a.reshape(C, C) for a in (q, k, v)] + [i["L0_attn_wg"].T], 1).reshape(KT, P, 4 * C)
    wo = tiles(i["L0_attn_wo"].T).reshape(1, P, KT * C)
    decay, rot = retention_tables()
    gn = np.stack([np.repeat(i[k], RD).reshape(KT, P).T for k in ("L0_attn_gn_weight", "L0_attn_gn_bias")], 1)
    blk = np.kron(np.eye(P // RD), np.full((RD, RD), 1.0 / RD)).astype(np.float32)
    return {"a_w": np.concatenate([w, wo], 0), "a_decay": decay, "a_rot": rot, "a_gn": gn, "a_blk": blk}


def layout_feed_forward(i):
    f1 = np.concatenate([i["L0_ffn_expert_fc1"].reshape(E * FE, C), i["L0_ffn_shared_fc1"]], 0)
    f2 = np.concatenate([i["L0_ffn_expert_fc2"].reshape(E * FE, C), i["L0_ffn_shared_fc2"]], 0)
    pr = np.concatenate([i["L0_ffn_expert_proj"].transpose(0, 2, 1).reshape(E * FE, C), i["L0_ffn_shared_proj"].T], 0)
    ups = [w.reshape(FT, P, KT, P).transpose(0, 3, 2, 1).reshape(FT, P, C) for w in (f1, f2)]
    w = np.concatenate(ups + [pr.reshape(FT, P, C)], 2)
    owner = np.minimum(np.arange(FT * P) // FE, E).reshape(FT, 1, P)
    sel = (owner == np.arange(16)[None, :, None]).astype(np.float32)
    sel = np.concatenate([sel, sel], 1)
    gates = np.zeros((C, P), np.float32)
    gates[:, :E] = i["L0_ffn_gate_w"].T
    gates[:, E] = i["L0_ffn_shared_gate_w"][0]
    key = np.tile(np.arange(E, 0, -1, dtype=np.float32), (P, 1))
    return {"c_w": w, "c_sel": sel, "c_gate": tiles(gates), "c_key": key}


def layout_attention(i):
    def apart(w):
        return w.reshape(-1, XH, 2, 4, 2).transpose(0, 4, 1, 2, 3).reshape(-1, C)

    kv = np.concatenate([apart(i["L0_xattn_Wkv"][:, :C]), i["L0_xattn_Wkv"][:, C:]], 1)
    w = np.stack([tiles(a).reshape(P, 2048) for a in (apart(i["L0_xattn_Wq"]), kv, i["L0_xattn_Wout"])])
    ctx = i["ctx_1024"].reshape(B, S, CKT, P).transpose(0, 3, 2, 1)
    pos = i["fside_BxSx2_0"].reshape(NT, P, 2).transpose(1, 0, 2)
    freq = np.tile(np.float32(10000.0) ** (-np.arange(4, dtype=np.float32) / np.float32(4)), (P, 2, 1)).astype(np.float32)
    bout = np.broadcast_to(i["L0_xattn_bout"], (P, C))
    return {"b_w": w, "b_ctx": ctx, "b_pos": pos, "b_freq": freq, "b_bout": bout}


def decoder_layer(nc, ins, out_dram):
    with ExitStack() as mem:
        X = mem.enter_context(nc.sbuf_tensor("residual", [P, NT, C], FP32))
        ident = mem.enter_context(nc.sbuf_tensor("identity", [P, P], FP32))
        retention(nc, X, ins["x"], ins["a_w"], ins["a_decay"], ins["a_rot"], ins["a_gn"], ins["a_blk"], ident, ins["ident"])
        cross_attention(nc, X, ins["b_w"], ins["b_ctx"], ins["b_pos"], ins["b_freq"], ins["b_bout"], ident)
        feed_forward(nc, X, ins["c_w"], ins["c_sel"], ins["c_gate"], ins["c_key"], ident, out_dram)


def kernel(**inputs):
    import concourse.bacc as bacc
    from concourse.bass_utils import run_bass_kernel_spmd

    i = {k: np.asarray(v) for k, v in inputs.items()}
    arrays = {"x": tiles(i["x"].reshape(B * S, C)), "ident": np.eye(P, dtype=np.float32)}
    arrays |= layout_retention(i) | layout_attention(i) | layout_feed_forward(i)
    nc = bacc.Bacc("TRN2", target_bir_lowering=False, num_devices=1)
    feeds, ins = {}, {}
    for name, a in arrays.items():
        feeds[f"in_{name}"] = np.ascontiguousarray(a)
        ins[name] = nc.dram_tensor(f"in_{name}", a.shape, mybir.dt.from_np(a.dtype), kind="ExternalInput").ap()
    out = nc.dram_tensor("out_0", (P, NT, C), FP32, kind="ExternalOutput").ap()
    decoder_layer(nc, ins, out)
    r = run_bass_kernel_spmd(nc, [feeds], core_ids=[0])
    return r.results[0]["out_0"].transpose(1, 0, 2).reshape(B, S, C)
```
